# Optimizing a Trainium2 kernel written in Bass

```python
import numpy as np
import jax
import jax.numpy as jnp

def _softmax(x, axis=-1):
    return jax.nn.softmax(x, axis=axis)

def _gelu(x):
    return jax.nn.gelu(x, approximate=True)

def _silu(x):
    return jax.nn.silu(x)

def _sigmoid(x):
    return jax.nn.sigmoid(x)

def _layernorm(x, axis=-1, eps=1e-05):
    m = jnp.mean(x, axis=axis, keepdims=True)
    v = jnp.var(x, axis=axis, keepdims=True)
    return (x - m) / jnp.sqrt(v + eps)

def _scatter_add(tgt, idx, src, axis=0):
    return tgt.at[idx].add(src)

def _segment_sum(src, seg, n):
    return jax.ops.segment_sum(src, seg, n)
kernel_name = 'mk_xattn_seq_d2_seqx_r8_2a8e5c'

def setup_inputs(seed: int=0):
    np.random.seed(seed)
    _w = jnp.asarray

    def _rec_inputs():
        import jax
        import jax.numpy as jnp
        _rk = jax.random.key(seed)
        x = -0.0005207 + 1.001 * jax.random.normal(jax.random.fold_in(_rk, 1), (128, 64, 128), jnp.float32)
        _lenS = 64 - jax.random.randint(jax.random.fold_in(_rk, 7), (128,), 0, max(1, 64 // 4) + 1, jnp.int32)
        _lenS2 = 64 - jax.random.randint(jax.random.fold_in(_rk, 8), (128,), 0, max(1, 64 // 4) + 1, jnp.int32)
        _ctx_768P = jax.random.normal(jax.random.fold_in(_rk, 11), (128, 16, 96), jnp.float32)
        _ctx_768c = jax.random.dirichlet(jax.random.fold_in(_rk, 511), 0.3 * jnp.ones((16,), jnp.float32), (128, 64))
        _ctx_768t = jnp.einsum('bsk,bkd->bsd', _ctx_768c, _ctx_768P)
        _ctx_768t = _ctx_768t * jax.lax.rsqrt(jnp.mean(jnp.square(_ctx_768t)) + 1e-12) * 0.953939
        ctx_768 = -0.0031663 + 0.998652 * (_ctx_768t + 0.3 * jax.random.normal(jax.random.fold_in(_rk, 611), (128, 64, 96), jnp.float32))
        _validS = jnp.arange(64)[None, :] < _lenS[:, None]
        _validS2 = jnp.arange(64)[None, :] < _lenS2[:, None]
        _causal = jnp.tril(jnp.ones((64, 64), dtype=bool))
        mask_BxS2_if1 = jnp.where(jnp.ones((128, 64), dtype=bool), 1, 0).astype(jnp.int32)
        return (x, ctx_768, mask_BxS2_if1)
    x, ctx_768, mask_BxS2_if1 = _rec_inputs()

    def _L0_xattn_setup():
        import jax, jax.numpy as jnp
        import numpy as np
        B, N, D = (1, 256, 128)
        H, DH = (16, 64)
        CN, CD = (77, 96)
        FF = 4 * D
        EPS = 1e-05
        SCALE = DH ** (-0.5)

        def layer_norm(x, g, b):
            mu = jnp.mean(x, axis=-1, keepdims=True)
            var = jnp.var(x, axis=-1, keepdims=True)
            return (x - mu) * jax.lax.rsqrt(var + EPS) * g + b

        def cross_attention(x, ctx, wq, wk, wv, wo, bo):
            b, n, _ = x.shape
            m = ctx.shape[1]
            q = (x @ wq.T).reshape(b, n, H, DH)
            k = (ctx @ wk.T).reshape(b, m, H, DH)
            v = (ctx @ wv.T).reshape(b, m, H, DH)
            sim = jnp.einsum('bihd,bjhd->bhij', q, k) * SCALE
            attn = jax.nn.softmax(sim, axis=-1)
            out = jnp.einsum('bhij,bjhd->bihd', attn, v).reshape(b, n, H * DH)
            return out @ wo.T + bo

        def geglu_ffn(x, w_geglu, b_geglu, w_ffout, b_ffout):
            proj = x @ w_geglu.T + b_geglu
            h, gate = (proj[..., :FF], proj[..., FF:])
            h = h * jax.nn.gelu(gate, approximate=False)
            return h @ w_ffout.T + b_ffout
        key = jax.random.key(seed)
        ks = jax.random.split(key, 24)
        s = 0.02
        n = lambda k, shape: jax.random.normal(k, shape, dtype=jnp.float32) * s
        return {'hidden_states': jax.random.normal(ks[0], (B, N, D), dtype=jnp.float32), 'context': jax.random.normal(ks[1], (B, CN, CD), dtype=jnp.float32), 'wq1': n(ks[2], (H * DH, D)), 'wk1': n(ks[3], (H * DH, D)), 'wv1': n(ks[4], (H * DH, D)), 'wo1': n(ks[5], (D, H * DH)), 'bo1': jnp.zeros((D,), jnp.float32), 'wq2': n(ks[6], (H * DH, D)), 'wk2': n(ks[7], (H * DH, CD)), 'wv2': n(ks[8], (H * DH, CD)), 'wo2': n(ks[9], (D, H * DH)), 'bo2': jnp.zeros((D,), jnp.float32), 'w_geglu': n(ks[10], (2 * FF, D)), 'b_geglu': jnp.zeros((2 * FF,), jnp.float32), 'w_ffout': n(ks[11], (D, FF)), 'b_ffout': jnp.zeros((D,), jnp.float32), 'ln1_g': jnp.ones((D,), jnp.float32), 'ln1_b': jnp.zeros((D,), jnp.float32), 'ln2_g': jnp.ones((D,), jnp.float32), 'ln2_b': jnp.zeros((D,), jnp.float32), 'ln3_g': jnp.ones((D,), jnp.float32), 'ln3_b': jnp.zeros((D,), jnp.float32)}
    _L0_xattn_all = _L0_xattn_setup()
    _L0_xattn_in = {k: v for k, v in _L0_xattn_all.items() if k in ('wq1', 'wk1', 'wv1', 'wo1', 'bo1', 'wq2', 'wk2', 'wv2', 'wo2', 'bo2', 'w_geglu', 'b_geglu', 'w_ffout', 'b_ffout', 'ln1_g', 'ln1_b', 'ln2_g', 'ln2_b', 'ln3_g', 'ln3_b')}
    del _L0_xattn_all

    def _L1_xattn_setup():
        import jax, jax.numpy as jnp
        import numpy as np
        import math
        H = 8
        D = 128
        D_I = 128
        D_L = 96
        EPS = 1e-05
        key = jax.random.key(seed)
        ks = jax.random.split(key, 8)
        B, NQ, NK = (8, 196, 128)
        img_embed = jax.random.normal(ks[0], (B, NQ, D_I), dtype=jnp.float32)
        sent_embed = jax.random.normal(ks[1], (B, NK, D_L), dtype=jnp.float32)
        atten_mask = jnp.ones((B, NK), dtype=jnp.int32)
        Wq = jax.random.normal(ks[2], (D_I, H * D), dtype=jnp.float32) * (1.0 / math.sqrt(D_I))
        Wk = jax.random.normal(ks[3], (D_L, H * D), dtype=jnp.float32) * (1.0 / math.sqrt(D_L))
        Wv = jax.random.normal(ks[4], (D_L, H * D), dtype=jnp.float32) * (1.0 / math.sqrt(D_L))
        Wo = jax.random.normal(ks[5], (H * D, D_I), dtype=jnp.float32) * (1.0 / math.sqrt(H * D))
        gamma = jnp.ones((D_I,), dtype=jnp.float32)
        beta = jnp.zeros((D_I,), dtype=jnp.float32)
        return {'img_embed': img_embed, 'sent_embed': sent_embed, 'atten_mask': atten_mask, 'Wq': Wq, 'Wk': Wk, 'Wv': Wv, 'Wo': Wo, 'gamma': gamma, 'beta': beta}
    _L1_xattn_all = _L1_xattn_setup()
    _L1_xattn_in = {k: v for k, v in _L1_xattn_all.items() if k in ('Wq', 'Wk', 'Wv', 'Wo', 'gamma', 'beta')}
    del _L1_xattn_all
    return {'x': x, 'ctx_768': ctx_768, 'mask_BxS2_if1': mask_BxS2_if1, 'L0_xattn_wq1': _L0_xattn_in['wq1'], 'L0_xattn_wk1': _L0_xattn_in['wk1'], 'L0_xattn_wv1': _L0_xattn_in['wv1'], 'L0_xattn_wo1': _L0_xattn_in['wo1'], 'L0_xattn_bo1': _L0_xattn_in['bo1'], 'L0_xattn_wq2': _L0_xattn_in['wq2'], 'L0_xattn_wk2': _L0_xattn_in['wk2'], 'L0_xattn_wv2': _L0_xattn_in['wv2'], 'L0_xattn_wo2': _L0_xattn_in['wo2'], 'L0_xattn_bo2': _L0_xattn_in['bo2'], 'L0_xattn_w_geglu': _L0_xattn_in['w_geglu'], 'L0_xattn_b_geglu': _L0_xattn_in['b_geglu'], 'L0_xattn_w_ffout': _L0_xattn_in['w_ffout'], 'L0_xattn_b_ffout': _L0_xattn_in['b_ffout'], 'L0_xattn_ln1_g': _L0_xattn_in['ln1_g'], 'L0_xattn_ln1_b': _L0_xattn_in['ln1_b'], 'L0_xattn_ln2_g': _L0_xattn_in['ln2_g'], 'L0_xattn_ln2_b': _L0_xattn_in['ln2_b'], 'L0_xattn_ln3_g': _L0_xattn_in['ln3_g'], 'L0_xattn_ln3_b': _L0_xattn_in['ln3_b'], 'L1_xattn_Wq': _L1_xattn_in['Wq'], 'L1_xattn_Wk': _L1_xattn_in['Wk'], 'L1_xattn_Wv': _L1_xattn_in['Wv'], 'L1_xattn_Wo': _L1_xattn_in['Wo'], 'L1_xattn_gamma': _L1_xattn_in['gamma'], 'L1_xattn_beta': _L1_xattn_in['beta']}

def reference(x, ctx_768, mask_BxS2_if1, L0_xattn_wq1, L0_xattn_wk1, L0_xattn_wv1, L0_xattn_wo1, L0_xattn_bo1, L0_xattn_wq2, L0_xattn_wk2, L0_xattn_wv2, L0_xattn_wo2, L0_xattn_bo2, L0_xattn_w_geglu, L0_xattn_b_geglu, L0_xattn_w_ffout, L0_xattn_b_ffout, L0_xattn_ln1_g, L0_xattn_ln1_b, L0_xattn_ln2_g, L0_xattn_ln2_b, L0_xattn_ln3_g, L0_xattn_ln3_b, L1_xattn_Wq, L1_xattn_Wk, L1_xattn_Wv, L1_xattn_Wo, L1_xattn_gamma, L1_xattn_beta):
    import jax
    import jax.numpy as jnp

    def _L0_xattn_ref(hidden_states, context, wq1, wk1, wv1, wo1, bo1, wq2, wk2, wv2, wo2, bo2, w_geglu, b_geglu, w_ffout, b_ffout, ln1_g, ln1_b, ln2_g, ln2_b, ln3_g, ln3_b):
        import jax, jax.numpy as jnp
        import numpy as np
        B, N, D = (1, 256, 128)
        H, DH = (16, 64)
        CN, CD = (77, 96)
        FF = 4 * D
        EPS = 1e-05
        SCALE = DH ** (-0.5)

        def layer_norm(x, g, b):
            mu = jnp.mean(x, axis=-1, keepdims=True)
            var = jnp.var(x, axis=-1, keepdims=True)
            return (x - mu) * jax.lax.rsqrt(var + EPS) * g + b

        def cross_attention(x, ctx, wq, wk, wv, wo, bo):
            b, n, _ = x.shape
            m = ctx.shape[1]
            q = (x @ wq.T).reshape(b, n, H, DH)
            k = (ctx @ wk.T).reshape(b, m, H, DH)
            v = (ctx @ wv.T).reshape(b, m, H, DH)
            sim = jnp.einsum('bihd,bjhd->bhij', q, k) * SCALE
            attn = jax.nn.softmax(sim, axis=-1)
            out = jnp.einsum('bhij,bjhd->bihd', attn, v).reshape(b, n, H * DH)
            return out @ wo.T + bo

        def geglu_ffn(x, w_geglu, b_geglu, w_ffout, b_ffout):
            proj = x @ w_geglu.T + b_geglu
            h, gate = (proj[..., :FF], proj[..., FF:])
            h = h * jax.nn.gelu(gate, approximate=False)
            return h @ w_ffout.T + b_ffout
        x = hidden_states
        x = cross_attention(layer_norm(x, ln1_g, ln1_b), layer_norm(x, ln1_g, ln1_b), wq1, wk1, wv1, wo1, bo1) + x
        x = cross_attention(layer_norm(x, ln2_g, ln2_b), context, wq2, wk2, wv2, wo2, bo2) + x
        x = geglu_ffn(layer_norm(x, ln3_g, ln3_b), w_geglu, b_geglu, w_ffout, b_ffout) + x
        return x

    def _L1_xattn_ref(img_embed, sent_embed, atten_mask, Wq, Wk, Wv, Wo, gamma, beta):
        import jax, jax.numpy as jnp
        import numpy as np
        import math
        H = 8
        D = 128
        D_I = 128
        D_L = 96
        EPS = 1e-05
        B = img_embed.shape[0]
        Q = (img_embed @ Wq).reshape(B, -1, H, D).transpose(0, 2, 1, 3)
        K = (sent_embed @ Wk).reshape(B, -1, H, D).transpose(0, 2, 1, 3)
        V = (sent_embed @ Wv).reshape(B, -1, H, D).transpose(0, 2, 1, 3)
        score = jnp.einsum('bhqd,bhkd->bhqk', Q, K) / math.sqrt(D)
        mask = (atten_mask != 0)[:, None, None, :]
        score = jnp.where(mask, score, -jnp.inf)
        attn = jax.nn.softmax(score, axis=-1)
        ctx = jnp.einsum('bhqk,bhkd->bqhd', attn, V).reshape(B, -1, H * D)
        out = ctx @ Wo + img_embed
        mu = jnp.mean(out, axis=-1, keepdims=True)
        var = jnp.var(out, axis=-1, keepdims=True)
        return (out - mu) * jax.lax.rsqrt(var + EPS) * gamma + beta
    x = _L0_xattn_ref(x, ctx_768, L0_xattn_wq1, L0_xattn_wk1, L0_xattn_wv1, L0_xattn_wo1, L0_xattn_bo1, L0_xattn_wq2, L0_xattn_wk2, L0_xattn_wv2, L0_xattn_wo2, L0_xattn_bo2, L0_xattn_w_geglu, L0_xattn_b_geglu, L0_xattn_w_ffout, L0_xattn_b_ffout, L0_xattn_ln1_g, L0_xattn_ln1_b, L0_xattn_ln2_g, L0_xattn_ln2_b, L0_xattn_ln3_g, L0_xattn_ln3_b)
    x = _L1_xattn_ref(x, ctx_768, mask_BxS2_if1, L1_xattn_Wq, L1_xattn_Wk, L1_xattn_Wv, L1_xattn_Wo, L1_xattn_gamma, L1_xattn_beta)
    return x

_drawn_inputs = setup_inputs


def setup_inputs(seed=0):
    import zlib

    import numpy as np

    out = dict(_drawn_inputs(seed))
    spreads = {'L0_xattn_bo1': (0.0, 0.1),
     'L0_xattn_bo2': (0.0, 0.1),
     'L0_xattn_b_geglu': (0.0, 0.8),
     'L0_xattn_b_ffout': (0.0, 0.301),
     'L0_xattn_ln1_g': (1.0, 0.6),
     'L0_xattn_ln1_b': (0.0, 0.572),
     'L0_xattn_ln2_g': (1.0, 0.6),
     'L0_xattn_ln2_b': (0.0, 0.8),
     'L0_xattn_ln3_g': (1.0, 0.6),
     'L0_xattn_ln3_b': (0.0, 0.8),
     'L1_xattn_gamma': (1.0, 0.2),
     'L1_xattn_beta': (0.0, 0.1)}
    factors = {'L0_xattn_wq1': 8.0,
     'L0_xattn_wk1': 8.0,
     'L0_xattn_wv1': 2.722,
     'L0_xattn_wo1': 2.676,
     'L0_xattn_wq2': 8.0,
     'L0_xattn_wk2': 8.0,
     'L0_xattn_w_geglu': 3.891,
     'L0_xattn_w_ffout': 3.823}
    for name, (base, spread) in spreads.items():
        noise = np.random.default_rng([zlib.crc32(name.encode()), seed]).standard_normal(out[name].shape)
        drawn = base * np.exp(spread * noise) if base else spread * noise
        out[name] = jnp.asarray(drawn.astype(out[name].dtype))
    for name, factor in factors.items():
        out[name] = (out[name] * factor).astype(out[name].dtype)
    return out
```

```python
from contextlib import ExitStack

import numpy as np
import concourse.bass as bass
from concourse import mybir
from concourse.alu_op_type import AluOpType as ALU

F32 = mybir.dt.float32
I32 = mybir.dt.int32
ACT = mybir.ActivationFunctionType
AX_X = mybir.AxisListType.X

P = 128
NB, SEQ, D = 128, 64, 128
CD = 96
BPG = 4
TOK = BPG * SEQ
TPG = TOK // P
NG = NB // BPG
TILES = NB * SEQ // P
FF = 4 * D
EPS = 1e-5
MASKED = -1e30


class Group:

    def __init__(self, base, i=None):
        self.base, self.i, self.par = base, i, base % 2

    def at(self, mult, add=0):
        c = mult * self.base + add
        return c if self.i is None else self.i * (2 * mult) + c

    def half(self, mult, add=0):
        c = mult * (self.base // 2) + add
        return c if self.i is None else self.i * mult + c

    def plus(self, n):
        return Group(self.base + n, self.i)

    def __bool__(self):
        return self.i is not None or 0 <= self.base < NG


def over_groups(eng, body, before_loop=None):
    for g in range(-2, 2):
        body(Group(g))
    if before_loop:
        before_loop()
    with eng.Fori(0, (NG - 4) // 2) as i:
        body(Group(2, i))
        body(Group(3, i))
    for g in range(NG - 2, NG + 2):
        body(Group(g))


def wait(eng, sem, value):
    if not isinstance(value, int) or value > 0:
        eng.wait_ge(sem, value)


class Attn:

    def __init__(self, name, heads, kw, ctx, ln, mask):
        self.name, self.heads, self.kw, self.ctx, self.ln, self.mask = name, heads, kw, ctx, ln, mask
        self.pairs = heads // 2
        self.turns = heads // 4
        self.ring = heads // 2 + 1
        self.srows = kw + 1 if mask else kw


SELF = Attn("self", 16, D, ctx=False, ln=True, mask=False)
CROSS = Attn("cross", 16, CD, ctx=True, ln=True, mask=False)
LAST = Attn("last", 8, CD, ctx=True, ln=False, mask=True)


def build(nc, t, out):
    with ExitStack() as stack:
        def sb(name, shape, dt=F32):
            return stack.enter_context(nc.sbuf_tensor(name, shape, dt))

        def sem(name):
            return stack.enter_context(nc.semaphore(name))

        ps_s = [stack.enter_context(nc.psum_tensor(f"ps_s{i}", [P, 512], F32)) for i in range(2)]
        ps_ring = [stack.enter_context(nc.psum_tensor(f"ps_ring{i}", [P, 512], F32)) for i in range(2)]
        ps_u = [stack.enter_context(nc.psum_tensor(f"ps_u{i}", [P, 512], F32)) for i in range(2)]
        ps_pt = stack.enter_context(nc.psum_tensor("ps_pt", [P, 512], F32))
        ps_o = stack.enter_context(nc.psum_tensor("ps_o", [P, 512], F32))

        x = sb("x_rows", [P, TILES, D])
        ident = sb("ident", [P, P])
        yt = sb("yt", [P, 2, BPG, 16 * SEQ])
        ut = sb("ut", [P, 2, 16, TOK])
        xrow = sb("xrow", [P, 2, TPG, D])
        crow = sb("crow", [P, 2, TPG, CD])
        cdup = sb("cdup", [P, 2, BPG, D])
        xt = sb("xt", [P, 2, TOK])
        kt = sb("kt", [P, 2, TOK])
        prob = sb("prob", [P, 2, 512])
        pt = sb("pt", [P, 2, 512])
        smax = sb("smax", [P, 2, 8])
        ssum = sb("ssum", [P, 2, 8])
        srec = sb("srec", [P, 2, 8])
        ot = sb("ot", [P, TOK])
        stats = sb("stats", [P, TPG, 6])
        moments = sb("moments", [P, TPG, 2])
        rstd = sb("rstd", [P, TPG])
        varp = sb("varp", [P, TPG])
        eps = sb("eps", [P, TPG])
        carrier = sb("carrier", [P, 1])
        mhalf = sb("mhalf", [P, TPG])
        orow = sb("orow", [P, 2, TPG, D])
        fold_qk = {a.name: sb(f"fold_qk_{a.name}", [P, a.heads, a.kw]) for a in (SELF, CROSS, LAST)}
        fold_vo = {a.name: sb(f"fold_vo_{a.name}", [P, a.heads, D]) for a in (SELF, CROSS, LAST)}
        wg_t = sb("wg_t", [P, 8, P])
        wf_t = sb("wf_t", [P, 4, P])
        gains = {n: sb(f"{n}_b", [P, D]) for n in ("ln1_g", "ln1_b", "ln2_g", "ln2_b", "ln3_g", "ln3_b", "gamma", "beta")}
        cols = sb("cols", [P, 11])
        row_eps = sb("row_eps", [P, TILES])
        raw_a = yt[:].rearrange("p a b c -> p (a b c)")
        raw_b = ut[:].rearrange("p a b c -> p (a b c)")

        jobs = []
        raws = []
        place = [0, 0]

        def raw(which, ap, rows, shape):
            n = int(np.prod(shape))
            base = (raw_a, raw_b)[which][0:rows, place[which]:place[which] + n]
            place[which] += n
            assert place[which] <= 8192
            names = " ".join("abc"[:len(shape)])
            view = base.rearrange(f"p ({names}) -> p {names}", **{"abc"[k]: shape[k] for k in range(len(shape))})
            raws.append((view, ap))
            return view, len(raws)

        def space(which, shape):
            n = int(np.prod(shape))
            base = (raw_a, raw_b)[which][:, place[which]:place[which] + n]
            place[which] += n
            assert place[which] <= 8192
            return base.rearrange("p (a b) -> p a b", a=shape[0])

        def bank(n):
            return ps_ring[n % 2]

        def turn4(src, rows, width, dst, loaded):
            n = len(jobs)
            ps = bank(n)[0:width, 0:4 * rows].rearrange("p (k r) -> p k r", k=4)
            jobs.append((loaded, 0, [(ps[:, k, :], "turn", src(k), rows) for k in range(4)], [(dst, ps, 1.0)]))
            return n + 1

        def prep_l0(wq, wk, wv, wo, a, which):
            wqr, l1 = raw(which, wq.rearrange("(t p) d -> p t d", p=P), P, [8, D])
            wkr, l2 = raw(which, wk.rearrange("(t p) d -> p t d", p=P), P, [8, a.kw])
            wvr, l3 = raw(which, wv.rearrange("(t p) d -> p t d", p=P), P, [8, a.kw])
            wor, l4 = raw(which, wo, P, [8, P])
            wot = space(which, [8, P])
            dep = 0
            for c in range(2):
                dep = turn4(lambda k, c=c: wor[:, 4 * c + k, :], P, P, wot[:, 4 * c:4 * c + 4, :], l4)
            for c in range(4):
                ps = bank(len(jobs))[:, 0:4 * a.kw].rearrange("p (k r) -> p k r", k=4)
                mm = []
                for k in range(4):
                    h = 8 * (c // 2) + 2 * k + c % 2
                    rows = slice(64 * (h % 2), 64 * (h % 2) + 64)
                    mm.append((ps[:, k, :], "mm", wqr[rows, h // 2, :], wkr[rows, h // 2, :]))
                jobs.append((l4, 0, mm, [(fold_qk[a.name][:, 8 * (c // 2) + c % 2:8 * (c // 2) + 8:2, :], ps, 64 ** -0.5)]))
            for c in range(4):
                ps = bank(len(jobs))[0:a.kw, :].rearrange("p (k r) -> p k r", k=4)
                mm = []
                for k in range(4):
                    h = 8 * (c // 2) + 2 * k + c % 2
                    rows = slice(64 * (h % 2), 64 * (h % 2) + 64)
                    mm.append((ps[:, k, :], "mm", wvr[rows, h // 2, :], wot[rows, h // 2, :]))
                jobs.append((l4, dep, mm, [(fold_vo[a.name][0:a.kw, 8 * (c // 2) + c % 2:8 * (c // 2) + 8:2, :], ps, 1.0)]))

        def prep_last():
            wqr, l1 = raw(0, t["L1_xattn_Wq"], P, [8, P])
            wkr, l2 = raw(0, t["L1_xattn_Wk"], CD, [8, P])
            wvr, l3 = raw(0, t["L1_xattn_Wv"], CD, [8, P])
            wor, l4 = raw(1, t["L1_xattn_Wo"].rearrange("(t p) d -> p t d", p=P), P, [8, P])
            wgr, l5 = raw(1, t["L0_xattn_w_geglu"].rearrange("(t p) d -> p t d", p=P), P, [8, P])
            wfr, l6 = raw(1, t["L0_xattn_w_ffout"], P, [4, P])
            wqt, wkt = space(0, [8, P]), space(0, [8, CD])
            wvt = space(0, [8, CD])
            for c in range(2):
                for src, rows, dst in ((wqr, P, wqt), (wkr, CD, wkt), (wvr, CD, wvt)):
                    dep = turn4(lambda k, c=c, src=src: src[:, 4 * c + k, :], rows, P, dst[:, 4 * c:4 * c + 4, :], l6)
            for c in range(2):
                ps = bank(len(jobs))[:, 0:4 * CD].rearrange("p (k r) -> p k r", k=4)
                jobs.append((l6, dep, [(ps[:, k, :], "mm", wqt[:, 4 * c + k, :], wkt[:, 4 * c + k, :]) for k in range(4)],
                             [(fold_qk["last"][:, 4 * c:4 * c + 4, :], ps, 128 ** -0.5)]))
            for c in range(2):
                ps = bank(len(jobs))[0:CD, :].rearrange("p (k r) -> p k r", k=4)
                jobs.append((l6, dep, [(ps[:, k, :], "mm", wvt[:, 4 * c + k, :], wor[:, 4 * c + k, :]) for k in range(4)],
                             [(fold_vo["last"][0:CD, 4 * c:4 * c + 4, :], ps, 1.0)]))
            for c in range(2):
                turn4(lambda k, c=c: wgr[:, 4 * c + k, :], P, P, wg_t[:, 4 * c:4 * c + 4, :], l6)
            turn4(lambda k: wfr[:, k, :], P, P, wf_t[:, :, :], l6)

        prep_l0(t["L0_xattn_wq1"], t["L0_xattn_wk1"], t["L0_xattn_wv1"], t["L0_xattn_wo1"], SELF, 0)
        first_raws = len(raws)
        prep_l0(t["L0_xattn_wq2"], t["L0_xattn_wk2"], t["L0_xattn_wv2"], t["L0_xattn_wo2"], CROSS, 1)
        second_raws, second_jobs = len(raws), len(jobs)
        place[:] = [0, 0]
        prep_last()

        s_ident = sem("s_ident")
        s_raw = [sem(f"s_raw{i}") for i in range(3)]
        s_small = sem("s_small")
        s_x = [sem("s_x_first"), sem("s_x_rest")]
        prep_ready = sem("prep_ready")
        prep_copied = sem("prep_copied")
        set_end = [first_raws, second_raws, len(raws)]
        set_sem = [0 if n < first_raws else 1 if n < second_raws else 2 for n in range(len(raws))]

        def raw_loaded(eng, n):
            k = set_sem[n - 1]
            eng.wait_ge(s_raw[k], 16 * (set_end[k] - (set_end[k - 1] if k else 0)))

        mask_i = sb("mask_i", [P, 2, TOK], I32)
        mask_h = sb("mask_h", [P, SEQ], I32)
        has_key = sb("has_key", [P, SEQ])
        any_key = sb("any_key", [P, 1])
        ones = sb("ones", [P, SEQ])
        key_sel = sb("key_sel", [P, 2, TILES])
        last_eps = sb("last_eps", [P, TILES])
        keys_spread = sem("keys_spread")
        s_ones_row = sem("s_ones_row")
        s_mask = sem("s_mask")
        s_bad = sem("s_bad")
        s_const = sem("s_const")

        phases = {}

        def phase_sems(name, names):
            phases[name] = {n: sem(f"{name}_{n}") for n in names}
            return phases[name]

        common = ["ring_done", "ring_free0", "ring_free1", "stat", "var_ready", "rstd_ready", "scaled_ready",
                  "norm_ready", "gain_done", "rows_ready", "o_done", "o_copied", "back_done", "resid_done"]
        attn = common + ["scores_done", "max_done", "shifted", "exp_done", "sum_done", "recip_done", "prob_ready",
                         "turned", "pt_copied", "u_done", "u_copied", "mask_done", "crow0", "crow1", "dup0", "dup1",
                         "mask0", "mask1", "out0", "out1", "fin_stat", "fin_var", "fin_rstd", "fin_norm",
                         "fin_gain", "fin_done"]
        sems = {"self": phase_sems("self", attn), "cross": phase_sems("cross", attn),
                "ffn": phase_sems("ffn", common + ["up_done", "gate_done", "h_done"]), "last": phase_sems("last", attn)}
        before = {"self": None, "cross": "self", "ffn": "cross", "last": "ffn"}

        def phase_begins(eng, name):
            if before[name]:
                eng.wait_ge(sems[before[name]]["resid_done"], NG)

        def ring_at(g, ring, k):
            n0 = ring * g.base + k
            uses = n0 // 2 if g.i is None else g.i * ring + n0 // 2
            return n0 % 2, uses

        block = stack.enter_context(nc.Block())

        @block.sync
        def _(sp):
            def load_set(k):
                lo = set_end[k - 1] if k else 0
                for view, ap in raws[lo:set_end[k]]:
                    dst = view
                    if len(ap.shape) == 2 and len(view.shape) == 3:
                        dst = view.rearrange("p a b -> p (a b)")
                    sp.dma_start(dst, ap).then_inc(s_raw[k], 16)

            xr = t["x"].rearrange("b s d -> (b s) d").rearrange("(t p) d -> p t d", p=P)
            cr = t["ctx_768"].rearrange("b s d -> (b s) d").rearrange("(t p) d -> p t d", p=P)
            orows = out.rearrange("b s d -> (b s) d").rearrange("(t p) d -> p t d", p=P)
            mr = t["mask_BxS2_if1"].rearrange("(a b) s -> a (b s)", a=1)
            first = 4 * TPG
            load_set(0)
            sp.dma_start(x[:, 0:first, :], xr[:, 0:first, :]).then_inc(s_x[0], 16)
            for n, src in (("ln1_g", "L0_xattn_ln1_g"), ("ln1_b", "L0_xattn_ln1_b"), ("ln2_g", "L0_xattn_ln2_g"),
                           ("ln2_b", "L0_xattn_ln2_b"), ("ln3_g", "L0_xattn_ln3_g"), ("ln3_b", "L0_xattn_ln3_b"),
                           ("gamma", "L1_xattn_gamma"), ("beta", "L1_xattn_beta")):
                sp.dma_start(gains[n][:], t[src].rearrange("(a d) -> a d", a=1).to_broadcast([P, D])).then_inc(s_small, 16)
            for c, n in enumerate(("L0_xattn_bo1", "L0_xattn_bo2", "L0_xattn_b_ffout")):
                sp.dma_start(cols[:, c:c + 1], t[n].rearrange("(d a) -> d a", a=1)).then_inc(s_small, 16)
            for c in range(8):
                sp.dma_start(cols[:, 3 + c:4 + c], t["L0_xattn_b_geglu"][c * P:(c + 1) * P].rearrange("(d a) -> d a", a=1)).then_inc(s_small, 16)
            load_set(1)
            sp.dma_start(x[:, first:TILES, :], xr[:, first:TILES, :]).then_inc(s_x[1], 16)
            sp.dma_start(mask_h[:], t["mask_BxS2_if1"]).then_inc(s_mask, 16)
            sp.wait_ge(prep_ready, second_jobs)
            load_set(2)

            for a in (SELF, CROSS, LAST):
                s = sems[a.name]
                phase_begins(sp, a.name)
                krow = crow if a.ctx else xrow

                def body(g):
                    nxt, dup, og = g.plus(2), g.plus(1), g.plus(-2)

                    def known(v):
                        return v if isinstance(v, int) else sp.snap(v)

                    dup_reads = known(dup.half(16, 16) if a.ctx else dup.at(1, 1))
                    dup_free = known(dup.at(2 * BPG, -2 * BPG))
                    if a.ctx:
                        tile, turned, copied = known(nxt.at(TPG)), known(g.at(a.ring, 1)), known(g.half(64, 64))
                    if a.mask:
                        token, masked = known(nxt.at(TOK)), known(g.at(1, 1))
                        otile, finished = known(og.at(TPG)), known(og.at(1, 1))

                    if nxt and a.ctx:
                        if g:
                            if g.i is None:
                                sp.wait_ge(s["ring_done"], turned)
                            sp.wait_ge(s[f"dup{g.par}"], copied)
                        sp.dma_start(crow[:, g.par, :, :], cr[:, bass.ds(tile, TPG), :]).then_inc(s[f"crow{g.par}"], 16)
                    if nxt and a.mask:
                        if g:
                            sp.wait_ge(s["mask_done"], masked)
                        sp.dma_start(mask_i[96:97, g.par, :], mr[:, bass.ds(token, TOK)]).then_inc(s[f"mask{g.par}"], 16)
                    if dup:
                        if dup.i is None:
                            sp.wait_ge(s[f"crow{dup.par}"] if a.ctx else s["rows_ready"], dup_reads)
                        if dup.i is not None or dup.base >= 2:
                            sp.wait_ge(s["u_done"], dup_free)
                        for r in range(2):
                            for b2 in range(2):
                                sp.dma_start(
                                    cdup[64 * r:64 * r + 64, dup.par, :, 0:a.kw].rearrange("p (t b) e -> p t b e", b=2)[:, :, b2, :],
                                    krow[64 * b2:64 * b2 + 64, dup.par, :, 0:a.kw]).then_inc(s[f"dup{dup.par}"], 16)
                    if og and a.mask:
                        sp.wait_ge(s["fin_done"], finished)
                        sp.dma_start(orows[:, bass.ds(otile, TPG), :], orow[:, og.par, :, :]).then_inc(s[f"out{og.par}"], 16)
                over_groups(sp, body)
            for p in range(2):
                sp.wait_ge(sems["last"][f"out{p}"], 16 * (NG // 2))

        @block.tensor
        def _(pe):
            pe.wait_ge(s_ident, 2)
            for n, (loaded, dep, mm, _) in enumerate(jobs):
                raw_loaded(pe, loaded)
                wait(pe, prep_copied, max(n - 1, dep))
                for o, kind, a, b in mm:
                    if kind == "turn":
                        last = pe.transpose(o, a, ident[0:b, 0:b])
                    else:
                        last = pe.matmul(o, a, b, start=True, stop=True)
                last.then_inc(prep_ready, 1)
            pe.wait_ge(s_bad, 5)
            for b2 in range(2):
                last = pe.matmul(ps_pt[64 * b2:64 * b2 + 64, 0:TILES], ones[:], key_sel[:, b2, :], start=True, stop=True)
            last.then_inc(keys_spread, 1)
            pe.wait_ge(s_bad, 6)
            pe.wait_ge(prep_copied, len(jobs))

            def turn_back(s, g):
                pe.wait_ge(s["o_copied"], g.at(1, 1))
                for k in range(TPG):
                    last = pe.transpose(ps_o[:, TOK + k * P:TOK + (k + 1) * P], ot[:, k * P:(k + 1) * P], ident[:, :])
                last.then_inc(s["back_done"], 1)

            def head_bank(s, g, ring, a):
                bank_, uses = ring_at(g, ring, 0)
                wait(pe, s[f"ring_free{bank_}"], uses)
                pe.wait_ge(s["rows_ready"], g.at(1, 1))
                for k in range(TPG):
                    last = pe.transpose(ps_ring[bank_][:, k * P:(k + 1) * P], xrow[:, g.par, k, :], ident[:, :])
                if a is not None and a.ctx:
                    pe.wait_ge(s[f"crow{g.par}"], g.half(16, 16))
                    for k in range(TPG):
                        last = pe.transpose(ps_ring[bank_][0:CD, TOK + k * P:TOK + (k + 1) * P], crow[:, g.par, k, :], ident[:, :])
                last.then_inc(s["ring_done"], 1)

            def attention(a):
                s = sems[a.name]
                wqk, wvo = fold_qk[a.name], fold_vo[a.name]
                keys = kt if a.ctx else xt
                per_step = a.pairs // 2

                def scores(g, b):
                    if b == 0:
                        for k in (a.pairs - 1, a.pairs):
                            bank_, uses = ring_at(g, a.ring, k)
                            pe.wait_ge(s[f"ring_free{bank_}"], uses + 1)
                        if a.mask:
                            pe.wait_ge(s["mask_done"], g.at(1, 1))
                            if g.i is None and g.base == 0:
                                pe.wait_ge(s_ones_row, 1)
                    wait(pe, s["shifted"], g.at(BPG, b - 1))
                    for q in range(a.pairs):
                        last = pe.matmul(ps_s[b % 2][:, q * SEQ:(q + 1) * SEQ],
                                         yt[0:a.srows, g.par, b, q * P:(q + 1) * P],
                                         keys[0:a.srows, g.par, b * SEQ:(b + 1) * SEQ], start=True, stop=True)
                    last.then_inc(s["scores_done"], 1)

                def queries(g, k):
                    bank_, uses = ring_at(g, a.ring, k + 1)
                    wait(pe, s[f"ring_free{bank_}"], uses)
                    if k == 0:
                        hb, huses = ring_at(g, a.ring, 0)
                        pe.wait_ge(s[f"ring_free{hb}"], huses + 1)
                    for j in range(2):
                        last = pe.matmul(ps_ring[bank_][0:a.kw, j * TOK:(j + 1) * TOK], wqk[:, 2 * k + j, :],
                                         xt[:, g.par, :], start=True, stop=True)
                    last.then_inc(s["ring_done"], 1)

                def turn_probs(g, b):
                    pe.wait_ge(s["prob_ready"], g.at(BPG, b + 1))
                    wait(pe, s["pt_copied"], g.at(BPG, b))
                    for k in range(a.turns):
                        last = pe.transpose(ps_pt[:, k * P:(k + 1) * P], prob[:, b % 2, k * P:(k + 1) * P], ident[:, :])
                    last.then_inc(s["turned"], 1)

                def mix(g, b):
                    pe.wait_ge(s["pt_copied"], g.at(BPG, b + 1))
                    if b == 0:
                        pe.wait_ge(s[f"dup{g.par}"], g.half(64, 64))
                    for r in range(2):
                        wait(pe, s["u_copied"], g.at(2 * BPG, 2 * b + r - 1))
                        pe.matmul(ps_u[r][0:a.kw, 0:a.turns * P], cdup[64 * r:64 * r + 64, g.par, b, 0:a.kw],
                                  pt[64 * r:64 * r + 64, b % 2, 0:a.turns * P], start=True, stop=True).then_inc(s["u_done"], 1)

                def project(g, part):
                    if part == 0:
                        pe.wait_ge(s["u_copied"], g.at(2 * BPG, 2 * BPG))
                        wait(pe, s["resid_done"], g.at(1))
                    half = a.heads // 2
                    for h in range(part * half, part * half + half):
                        last = pe.matmul(ps_o[:, 0:TOK], wvo[0:a.kw, h, :], ut[0:a.kw, g.par, h, :],
                                         start=(h == 0), stop=(h == a.heads - 1))
                    if part == 1:
                        last.then_inc(s["o_done"], 1)

                def body(g):
                    for b in range(BPG):
                        if g:
                            scores(g, b)
                        if b < 2 and g.plus(1):
                            for k in range(b * per_step, (b + 1) * per_step):
                                queries(g.plus(1), k)
                        if b >= 2 and g.plus(-1):
                            project(g.plus(-1), b - 2)
                        tg, tb = (g, b - 1) if b >= 1 else (g.plus(-1), BPG - 1)
                        if tg:
                            turn_probs(tg, tb)
                        ug, ub = (g, b - 2) if b >= 2 else (g.plus(-1), b + 2)
                        if ug:
                            mix(ug, ub)
                        if b == 0 and g.plus(-2):
                            turn_back(s, g.plus(-2))
                        if b == BPG - 1 and g.plus(2):
                            head_bank(s, g.plus(2), a.ring, a)
                over_groups(pe, body)

            def ffn():
                s = sems["ffn"]

                def up(g):
                    hb, huses = ring_at(g, 1, 0)
                    pe.wait_ge(s[f"ring_free{hb}"], huses + 1)
                    for c in range(4):
                        dst = (ps_s[0], ps_s[1], ps_u[0], ps_u[1])[c]
                        wait(pe, s["h_done"], g.at(4, c - 3))
                        pe.matmul(dst[:, 0:TOK], wg_t[:, 4 + c, :], xt[:, g.par, :], start=True, stop=True)
                        pe.matmul(dst[:, TOK:2 * TOK], wg_t[:, c, :], xt[:, g.par, :], start=True, stop=True)\
                          .then_inc(s["up_done"], 1)

                def down(g):
                    pe.wait_ge(s["h_done"], g.at(4, 4))
                    wait(pe, s["resid_done"], g.at(1))
                    for c in range(4):
                        last = pe.matmul(ps_o[:, 0:TOK], wf_t[:, c, :], ut[:, g.par, c, :], start=(c == 0), stop=(c == 3))
                    last.then_inc(s["o_done"], 1)

                def body(g):
                    if g.plus(-1):
                        down(g.plus(-1))
                    if g.plus(1):
                        up(g.plus(1))
                    if g.plus(2):
                        head_bank(s, g.plus(2), 1, None)
                    if g.plus(-1):
                        turn_back(s, g.plus(-1))
                over_groups(pe, body)

            for name, run in (("self", lambda: attention(SELF)), ("cross", lambda: attention(CROSS)),
                              ("ffn", ffn), ("last", lambda: attention(LAST))):
                phase_begins(pe, name)
                run()

        def ring_out(eng, copy, s, g, a, k):
            ring = a.ring if a else 1
            bank_, uses = ring_at(g, ring, k)
            eng.wait_ge(s["ring_done"], g.at(ring, k + 1))
            ps = ps_ring[bank_]
            if k == 0:
                ins = copy(xt[:, g.par, :], ps[:, 0:TOK])
                if a and a.ctx:
                    ins = copy(kt[0:CD, g.par, :], ps[0:CD, TOK:2 * TOK])
            else:
                ins = copy(yt[0:a.kw, g.par, :, (2 * k - 2) * SEQ:2 * k * SEQ].rearrange("p b (h i) -> p b h i", h=2),
                           ps[0:a.kw, :].rearrange("p (h b i) -> p b h i", h=2, b=BPG))
            ins.then_inc(s[f"ring_free{bank_}"], 1)

        def ring_step(eng, copy, s, g, b, a, mine):
            if a is None:
                return
            per_step = a.pairs // 2
            if b < 2 and g.plus(1):
                for k in range(b * per_step + 1, (b + 1) * per_step + 1):
                    if ring_at(g.plus(1), a.ring, k)[0] == mine:
                        ring_out(eng, copy, s, g.plus(1), a, k)

        def head_step(eng, copy, s, g, a, mine):
            if g.plus(2) and ring_at(g.plus(2), a.ring if a else 1, 0)[0] == mine:
                ring_out(eng, copy, s, g.plus(2), a, 0)

        @block.scalar
        def _(act):
            def copy(dst, src):
                return act.activation(dst, src, ACT.Copy)

            def o_out(s, g, bias):
                act.wait_ge(s["o_done"], g.at(1, 1))
                wait(act, s["back_done"], g.at(1))
                if bias is None:
                    ins = copy(ot[:], ps_o[:, 0:TOK])
                else:
                    ins = act.activation(ot[:], ps_o[:, 0:TOK], ACT.Identity, bias=bias)
                ins.then_inc(s["o_copied"], 1)

            for n, (_, _, _, outs) in enumerate(jobs):
                if n % 2:
                    act.wait_ge(prep_ready, n + 1)
                    act.wait_ge(prep_copied, n)
                    for dst, src, scale in outs:
                        ins = act.activation(dst, src, ACT.Copy, scale=scale)
                    ins.then_inc(prep_copied, 1)
            act.wait_ge(s_small, 16 * 19)

            def attention(a, bias):
                s = sems[a.name]

                def body(g):
                    for b in range(BPG):
                        if g:
                            act.wait_ge(s["shifted"], g.at(BPG, b + 1))
                            act.activation(prob[:, b % 2, 0:a.pairs * SEQ], prob[:, b % 2, 0:a.pairs * SEQ], ACT.Exp)\
                               .then_inc(s["exp_done"], 1)
                        ring_step(act, copy, s, g, b, a, 1)
                        tg, tb = (g, b - 1) if b >= 1 else (g.plus(-1), BPG - 1)
                        if tg:
                            act.wait_ge(s["turned"], tg.at(BPG, tb + 1))
                            copy(pt[:, tb % 2, 0:a.turns * P], ps_pt[:, 0:a.turns * P]).then_inc(s["pt_copied"], 1)
                        ug, ub = (g, b - 2) if b >= 2 else (g.plus(-1), b + 2)
                        if ug:
                            for r in range(2):
                                act.wait_ge(s["u_done"], ug.at(2 * BPG, 2 * ub + r + 1))
                                if ub == 0 and r == 0:
                                    wait(act, s["o_done"], ug.at(1, -1))
                                copy(ut[0:a.kw, ug.par, 0:a.heads, ub * SEQ:(ub + 1) * SEQ].rearrange(
                                        "e (t r k) i -> e t r k i", r=2, k=2)[:, :, r, :, :],
                                     ps_u[r][0:a.kw, 0:a.turns * P].rearrange("e (t k i) -> e t k i", k=2, i=SEQ))\
                                    .then_inc(s["u_copied"], 1)
                    if g.plus(-1):
                        o_out(s, g.plus(-1), bias)
                    head_step(act, copy, s, g, a, 1)
                over_groups(act, body)

            def ffn():
                s = sems["ffn"]

                def body(g):
                    if g.plus(-1):
                        o_out(s, g.plus(-1), cols[:, 2:3])
                    if g.plus(1):
                        n = g.plus(1)
                        for c in range(4):
                            act.wait_ge(s["up_done"], n.at(4, c + 1))
                            wait(act, s["h_done"], n.at(4, c - 3))
                            act.activation(yt[:, 0, c, 0:TOK], (ps_s[0], ps_s[1], ps_u[0], ps_u[1])[c][:, 0:TOK],
                                           ACT.Gelu, bias=cols[:, 7 + c:8 + c]).then_inc(s["gate_done"], 1)
                    head_step(act, copy, s, g, None, 1)
                over_groups(act, body)

            for name, run in (("self", lambda: attention(SELF, cols[:, 0:1])), ("cross", lambda: attention(CROSS, cols[:, 1:2])),
                              ("ffn", ffn), ("last", lambda: attention(LAST, None))):
                phase_begins(act, name)
                run()

        @block.vector
        def _(dve):
            def copy(dst, src):
                return dve.tensor_copy(dst, src)

            dve.memset(mhalf[:], -0.5).then_inc(s_const, 1)
            dve.memset(eps[:], EPS).then_inc(s_const, 1)
            for n, (_, _, _, outs) in enumerate(jobs):
                if n % 2 == 0:
                    dve.wait_ge(prep_ready, n + 1)
                    wait(dve, prep_copied, n)
                    for dst, src, scale in outs:
                        ins = dve.tensor_scalar(dst, src, scale, None, ALU.mult)
                    ins.then_inc(prep_copied, 1)
            dve.wait_ge(s_mask, 16)
            dve.tensor_scalar(has_key[:], mask_h[:], 0.0, None, ALU.not_equal).then_inc(s_bad, 1)
            dve.wait_ge(s_bad, 1)
            dve.tensor_reduce(any_key[:], has_key[:], AX_X, ALU.max).then_inc(s_bad, 1)
            dve.memset(ones[:], 1.0).then_inc(s_bad, 1)
            dve.wait_ge(s_bad, 3)
            dve.wait_ge(s_ident, 2)
            for b2 in range(2):
                dve.tensor_scalar(key_sel[:, b2, :], ident[:, b2:P:2], any_key[:, 0:1], None, ALU.mult).then_inc(s_bad, 1)
            dve.wait_ge(keys_spread, 1)
            dve.tensor_scalar(last_eps[:], ps_pt[:, 0:TILES], 0.0, -3e38, ALU.is_equal, ALU.mult).then_inc(s_bad, 1)
            dve.wait_ge(s_bad, 6)
            dve.tensor_scalar(row_eps[:], last_eps[:], 10.0, None, ALU.mult).then_inc(s_bad, 1)
            dve.wait_ge(s_bad, 7)
            dve.tensor_tensor(last_eps[:], row_eps[:], row_eps[:], ALU.subtract).then_inc(s_bad, 1)
            dve.wait_ge(s_bad, 8)
            dve.tensor_scalar(row_eps[:], last_eps[:], EPS, None, ALU.add).then_inc(s_bad, 1)
            dve.wait_ge(s_x[0], 16)
            dve.wait_ge(s_small, 16 * 19)

            def norm_stats(s, g, src, stat, var):
                for k in range(TPG):
                    dve.bn_stats(stats[:, k, :], src(k)).then_inc(s[stat], 1)
                dve.wait_ge(s[stat], g.at(TPG + 1, TPG))
                dve.memset(carrier[:], 0.0).then_inc(s[stat], 1)
                for k in range(TPG):
                    ins = dve.bn_aggr(moments[:, k, :], stats[:, k, :])
                ins.then_inc(s[var], 1)

            def norm_rows(s, g, src, dst, rst, done):
                dve.wait_ge(s[rst], g.at(1, 1))
                for k in range(TPG):
                    ins = dve.tensor_scalar(dst(k), src(k), moments[:, k, 0:1], rstd[:, k:k + 1], ALU.subtract, ALU.mult)
                ins.then_inc(s[done], 1)

            def ln_stats(s, g):
                norm_stats(s, g, lambda k: x[:, bass.ds(g.at(TPG, k), 1), :].rearrange("p a d -> p (a d)"), "stat", "var_ready")

            def ln_rows(s, g, ring, dup):
                if g.i is not None or g.base >= 2:
                    dve.wait_ge(s["ring_done"], g.at(ring, 1 - 2 * ring))
                    if dup:
                        dve.wait_ge(s[f"dup{g.par}"], g.half(64))
                norm_rows(s, g, lambda k: x[:, bass.ds(g.at(TPG, k), 1), :].rearrange("p a d -> p (a d)"),
                          lambda k: xrow[:, g.par, k, :], "rstd_ready", "norm_ready")

            def residual(s, g):
                dve.wait_ge(s["back_done"], g.at(1, 1))
                xs = x[:, bass.ds(g.at(TPG), TPG), :].rearrange("p t d -> p (t d)")
                dve.tensor_tensor(xs, ps_o[:, TOK:2 * TOK], xs, ALU.add).then_inc(s["resid_done"], 1)

            def final_rows(s, g):
                dve.wait_ge(s["back_done"], g.at(1, 1))
                if g.i is not None or g.base >= 2:
                    dve.wait_ge(s[f"out{g.par}"], g.half(16))
                o = orow[:, g.par, :, :].rearrange("p t d -> p (t d)")
                xs = x[:, bass.ds(g.at(TPG), TPG), :].rearrange("p t d -> p (t d)")
                dve.tensor_tensor(o, ps_o[:, TOK:2 * TOK], xs, ALU.add).then_inc(s["resid_done"], 1)
                dve.wait_ge(s["resid_done"], g.at(1, 1))
                norm_stats(s, g, lambda k: orow[:, g.par, k, :], "fin_stat", "fin_var")

            def final_norm(s, g):
                norm_rows(s, g, lambda k: orow[:, g.par, k, :], lambda k: orow[:, g.par, k, :], "fin_rstd", "fin_norm")

            def attention(a):
                s = sems[a.name]
                n = a.pairs * SEQ

                def body(g):
                    for b in range(BPG):
                        if g:
                            pb = prob[:, b % 2, 0:n].rearrange("p (q j) -> p q j", j=SEQ)
                            ps = ps_s[b % 2][:, 0:n].rearrange("p (q j) -> p q j", j=SEQ)
                            dve.wait_ge(s["scores_done"], g.at(BPG, b + 1))
                            dve.tensor_reduce(smax[:, b % 2, 0:a.pairs], ps, AX_X, ALU.max).then_inc(s["max_done"], 1)
                            dve.wait_ge(s["max_done"], g.at(BPG, b + 1))
                            wait(dve, s["turned"], g.at(BPG, b - 1))
                            dve.tensor_tensor(pb, ps, smax[:, b % 2, 0:a.pairs].unsqueeze(2).to_broadcast([P, a.pairs, SEQ]),
                                              ALU.subtract).then_inc(s["shifted"], 1)
                        ring_step(dve, copy, s, g, b, a, 0)
                        if b == 1 and g.plus(-2):
                            if a.mask:
                                final_rows(s, g.plus(-2))
                            else:
                                residual(s, g.plus(-2))
                        if b == 2 and g.plus(-2) and a.mask:
                            final_norm(s, g.plus(-2))
                        if g:
                            dve.wait_ge(s["exp_done"], g.at(BPG, b + 1))
                            dve.tensor_reduce(ssum[:, b % 2, 0:a.pairs], pb, AX_X, ALU.add).then_inc(s["sum_done"], 1)
                            dve.wait_ge(s["sum_done"], g.at(BPG, b + 1))
                            dve.reciprocal(srec[:, b % 2, 0:a.pairs], ssum[:, b % 2, 0:a.pairs]).then_inc(s["recip_done"], 1)
                        if b == 1 and g.plus(2) and a.ln:
                            ln_stats(s, g.plus(2))
                        if b == 2 and g.plus(2) and a.ln:
                            ln_rows(s, g.plus(2), a.ring, not a.ctx)
                    nxt = g.plus(2)
                    if nxt and a.mask:
                        dve.wait_ge(s[f"mask{nxt.par}"], nxt.half(16, 16))
                        if g:
                            dve.wait_ge(s["scores_done"], g.at(BPG, BPG))
                        dve.tensor_scalar(kt[96:97, g.par, :], mask_i[96:97, g.par, :], 0.0, MASKED,
                                          ALU.is_equal, ALU.mult).then_inc(s["mask_done"], 1)
                    head_step(dve, copy, s, g, a, 0)
                over_groups(dve, body, (lambda: dve.wait_ge(s_x[1], 16)) if a is SELF else None)

            def ffn():
                s = sems["ffn"]

                def body(g):
                    if g.plus(2):
                        ln_stats(s, g.plus(2))
                    if g.plus(-2):
                        residual(s, g.plus(-2))
                    if g.plus(2):
                        ln_rows(s, g.plus(2), 1, False)
                    if g.plus(1):
                        n = g.plus(1)
                        for c in range(4):
                            dve.wait_ge(s["gate_done"], n.at(4, c + 1))
                            if c == 0:
                                wait(dve, s["o_done"], n.at(1, -1))
                            dve.scalar_tensor_tensor(out=ut[:, n.par, c, :], in0=(ps_s[0], ps_s[1], ps_u[0], ps_u[1])[c][:, TOK:2 * TOK],
                                                     scalar=cols[:, 3 + c:4 + c], in1=yt[:, 0, c, 0:TOK],
                                                     op0=ALU.add, op1=ALU.mult).then_inc(s["h_done"], 1)
                    head_step(dve, copy, s, g, None, 0)
                over_groups(dve, body)

            for name, run in (("self", lambda: attention(SELF)), ("cross", lambda: attention(CROSS)),
                              ("ffn", ffn), ("last", lambda: attention(LAST))):
                phase_begins(dve, name)
                run()

        @block.gpsimd
        def _(pool):
            pool.memset(ident[:], 0.0).then_inc(s_ident, 1)
            pool.wait_ge(s_ident, 1)
            pool.affine_select(out=ident[:], in_=ident[:], compare_op=ALU.not_equal, fill=1.0, base=0,
                               pattern=[[-1, P]], channel_multiplier=1).then_inc(s_ident, 1)
            pool.wait_ge(s_const, 2)
            pool.wait_ge(s_small, 16 * 19)
            pool.wait_ge(s_bad, 9)

            def root(s, g, var, scaled, rst, row_eps=None):
                pool.wait_ge(s[var], g.at(1, 1))
                e = eps[:] if row_eps is None else row_eps[:, bass.ds(g.at(TPG), TPG)]
                pool.tensor_tensor(varp[:], moments[:, :, 1], e, ALU.add).then_inc(s[scaled], 1)
                pool.wait_ge(s[scaled], g.at(1, 1))
                pool.tensor_tensor(rstd[:], varp[:], mhalf[:], ALU.pow).then_inc(s[rst], 1)

            def affine(s, g, rows, gain, bias, norm, gained, done):
                pool.wait_ge(s[norm], g.at(1, 1))
                pool.tensor_tensor(rows, rows, gain[:].unsqueeze(1).to_broadcast([P, TPG, D]), ALU.mult).then_inc(s[gained], 1)
                pool.wait_ge(s[gained], g.at(1, 1))
                pool.tensor_tensor(rows, rows, bias[:].unsqueeze(1).to_broadcast([P, TPG, D]), ALU.add).then_inc(s[done], 1)

            def attention(a, gain, bias):
                s = sems[a.name]
                n = a.pairs * SEQ
                if a.mask:
                    pool.memset(yt[96:97, :, :, :], 1.0).then_inc(s_ones_row, 1)
                    pool.wait_ge(s_ones_row, 1)

                def body(g):
                    nxt = g.plus(2)
                    for b in range(BPG):
                        if g:
                            pool.wait_ge(s["recip_done"], g.at(BPG, b + 1))
                            pb = prob[:, b % 2, 0:n].rearrange("p (q j) -> p q j", j=SEQ)
                            pool.tensor_tensor(pb, pb, srec[:, b % 2, 0:a.pairs].unsqueeze(2).to_broadcast([P, a.pairs, SEQ]),
                                               ALU.mult).then_inc(s["prob_ready"], 1)
                        if a.mask and g.plus(-2):
                            og = g.plus(-2)
                            if b == 1:
                                root(s, og, "fin_var", "scaled_ready", "fin_rstd", row_eps)
                            if b == 2:
                                affine(s, og, orow[:, og.par, :, :], gain, bias, "fin_norm", "fin_gain", "fin_done")
                        if nxt and a.ln and b == 1:
                            root(s, nxt, "var_ready", "scaled_ready", "rstd_ready")
                        if nxt and a.ln and b == 2:
                            affine(s, nxt, xrow[:, g.par, :, :], gain, bias, "norm_ready", "gain_done", "rows_ready")
                        if nxt and not a.ln and b == 2:
                            if g:
                                pool.wait_ge(s["ring_done"], g.at(a.ring, 1))
                            pool.tensor_copy(xrow[:, g.par, :, :], x[:, bass.ds(nxt.at(TPG), TPG), :]).then_inc(s["rows_ready"], 1)
                over_groups(pool, body)

            def ffn():
                s = sems["ffn"]

                def body(g):
                    if g.plus(2):
                        root(s, g.plus(2), "var_ready", "scaled_ready", "rstd_ready")
                        affine(s, g.plus(2), xrow[:, g.par, :, :], gains["ln3_g"], gains["ln3_b"], "norm_ready", "gain_done", "rows_ready")
                over_groups(pool, body)

            for name, run in (("self", lambda: attention(SELF, gains["ln1_g"], gains["ln1_b"])),
                              ("cross", lambda: attention(CROSS, gains["ln2_g"], gains["ln2_b"])),
                              ("ffn", ffn), ("last", lambda: attention(LAST, gains["gamma"], gains["beta"]))):
                phase_begins(pool, name)
                run()


INPUTS = ["x", "ctx_768", "mask_BxS2_if1", "L0_xattn_wq1", "L0_xattn_wk1", "L0_xattn_wv1", "L0_xattn_wo1", "L0_xattn_bo1",
          "L0_xattn_wq2", "L0_xattn_wk2", "L0_xattn_wv2", "L0_xattn_wo2", "L0_xattn_bo2", "L0_xattn_w_geglu",
          "L0_xattn_b_geglu", "L0_xattn_w_ffout", "L0_xattn_b_ffout", "L0_xattn_ln1_g", "L0_xattn_ln1_b",
          "L0_xattn_ln2_g", "L0_xattn_ln2_b", "L0_xattn_ln3_g", "L0_xattn_ln3_b", "L1_xattn_Wq", "L1_xattn_Wk",
          "L1_xattn_Wv", "L1_xattn_Wo", "L1_xattn_gamma", "L1_xattn_beta"]


def kernel(**inputs):
    import numpy as _np
    import concourse.bacc as _bacc
    from concourse import mybir as _mybir
    from concourse.bass_utils import run_bass_kernel_spmd as _run

    nc = _bacc.Bacc("TRN2", target_bir_lowering=False, num_devices=1)
    arrays, handles = {}, {}
    for name in INPUTS:
        a = _np.ascontiguousarray(inputs[name])
        arrays[f"in_{name}"] = a
        handles[name] = nc.dram_tensor(f"in_{name}", a.shape, _mybir.dt.from_np(a.dtype), kind="ExternalInput").ap()
    out = nc.dram_tensor("out_rows", (NB, SEQ, D), F32, kind="ExternalOutput").ap()
    build(nc, handles, out)
    r = _run(nc, [arrays], core_ids=[0])
    return r.results[0]["out_rows"]
```

```python
from contextlib import ExitStack

import numpy as np
import concourse.bass as bass
from concourse import mybir
from concourse.alu_op_type import AluOpType as ALU

F32 = mybir.dt.float32
F32R = mybir.dt.float32r
I32 = mybir.dt.int32
ACT = mybir.ActivationFunctionType
AX_X = mybir.AxisListType.X

P = 128
NB, SEQ, D = 128, 64, 128
CD = 96
BPG = 4
TOK = BPG * SEQ
TPG = TOK // P
NG = NB // BPG
TILES = NB * SEQ // P
FF = 4 * D
EPS = 1e-5
MASKED = -1e30


class Group:

    def __init__(self, base, i=None):
        self.base, self.i, self.par = base, i, base % 2

    def at(self, mult, add=0):
        c = mult * self.base + add
        return c if self.i is None else self.i * (2 * mult) + c

    def half(self, mult, add=0):
        c = mult * (self.base // 2) + add
        return c if self.i is None else self.i * mult + c

    def plus(self, n):
        return Group(self.base + n, self.i)

    def __bool__(self):
        return self.i is not None or 0 <= self.base < NG


def over_groups(eng, body, lead=2, before_loop=None):
    end = (NG - lead) // 2 * 2
    for g in range(-lead, 2):
        body(Group(g))
    if before_loop:
        before_loop()
    with eng.Fori(0, (end - 2) // 2) as i:
        body(Group(2, i))
        body(Group(3, i))
    for g in range(end, NG + 2):
        body(Group(g))


def back(g, b, n):
    return (g, b - n) if b >= n else (g.plus(-1), b - n + BPG)


def matmul3(pe, out, w, v, start=True, stop=True):
    (w_hi, w_lo), (v_hi, v_lo) = w, v
    pe.matmul(out, w_lo, v_hi, start=start, stop=False)
    pe.matmul(out, w_hi, v_lo, start=False, stop=False)
    return pe.matmul(out, w_hi, v_hi, start=False, stop=stop)


def wait(eng, sem, value):
    if not isinstance(value, int) or value > 0:
        eng.wait_ge(sem, value)


class Attn:

    def __init__(self, name, heads, kw, ctx, ln, mask):
        self.name, self.heads, self.kw, self.ctx, self.ln, self.mask = name, heads, kw, ctx, ln, mask
        self.pairs = heads // 2
        self.turns = heads // 4
        self.ring = heads // 2 + 1
        self.srows = kw + 1 if mask else kw


SELF = Attn("self", 16, D, ctx=False, ln=True, mask=False)
CROSS = Attn("cross", 16, CD, ctx=True, ln=True, mask=False)
LAST = Attn("last", 8, CD, ctx=True, ln=False, mask=True)


def build(nc, t, out):
    with ExitStack() as stack:
        def sb(name, shape, dt=F32):
            return stack.enter_context(nc.sbuf_tensor(name, shape, dt))

        def sem(name):
            return stack.enter_context(nc.semaphore(name))

        ps_s = [stack.enter_context(nc.psum_tensor(f"ps_s{i}", [P, 512], F32)) for i in range(2)]
        ps_ring = [stack.enter_context(nc.psum_tensor(f"ps_ring{i}", [P, 512], F32)) for i in range(2)]
        ps_u = [stack.enter_context(nc.psum_tensor(f"ps_u{i}", [P, 512], F32)) for i in range(2)]
        ps_pt = stack.enter_context(nc.psum_tensor("ps_pt", [P, 512], F32))
        ps_o = stack.enter_context(nc.psum_tensor("ps_o", [P, 512], F32))

        ps_down = [ps_o, ps_pt]

        x = sb("x_rows", [P, TILES, D])
        ident = sb("ident", [P, P])
        yt = sb("yt", [P, 2, BPG, 16 * SEQ])
        ut = sb("ut", [P, 2, 16, TOK])
        xrow = sb("xrow", [P, 2, TPG, D])
        crow = sb("crow", [P, 2, TPG, CD])
        krow = [sb(f"krow_{n}", [P, 2, TPG, D], F32R) for n in ("hi", "lo")]
        cdup = [sb(f"cdup_{n}", [P, 2, BPG, D], F32R) for n in ("hi", "lo")]
        xt = [sb(f"xt_{n}", [P, 2, TOK], F32R) for n in ("hi", "lo")]
        kt = sb("kt", [P, 2, TOK])
        prob = sb("prob", [P, BPG, 512])
        pt = [sb(f"pt_{n}", [P, 2, 512], F32R) for n in ("first", "second")]
        smax = sb("smax", [P, BPG, 8])
        ssum = sb("ssum", [P, BPG, 8])
        srec = sb("srec", [P, BPG, 8])
        ot = sb("ot", [P, TOK])
        stats = sb("stats", [P, TPG, 6])
        moments = sb("moments", [P, TPG, 2])
        rstd = sb("rstd", [P, TPG])
        varp = sb("varp", [P, TPG])
        eps = sb("eps", [P, TPG])
        zero = sb("zero", [P, 1])
        carrier = sb("carrier", [P, 1])
        mhalf = sb("mhalf", [P, TPG])
        orow = ut[:, :, 8, :].rearrange("p n (t d) -> p n t d", d=D)
        mask_i = ut[:, :, 9, :].bitcast(I32)
        fold_qk = {a.name: [sb(f"fold_qk_{a.name}_{n}", [P, a.heads, a.kw], F32R) for n in ("hi", "lo")]
                   for a in (SELF, CROSS, LAST)}
        fold_vo = {a.name: sb(f"fold_vo_{a.name}", [P, a.heads, D]) for a in (SELF, CROSS, LAST)}
        wg_t = [sb(f"wg_t_{n}", [P, 8, P], F32R) for n in ("hi", "lo")]
        wf_t = sb("wf_t", [P, 4, P])
        gains = {n: sb(f"{n}_b", [P, D]) for n in ("ln1_g", "ln1_b", "ln2_g", "ln2_b", "ln3_g", "ln3_b", "gamma", "beta")}
        cols = sb("cols", [P, 11])
        row_eps = sb("row_eps", [P, TILES])
        raw_a = yt[:].rearrange("p a b c -> p (a b c)")
        raw_b = ut[:].rearrange("p a b c -> p (a b c)")

        jobs = []
        raws = []
        place = [0, 0]

        def raw(which, ap, rows, shape):
            n = int(np.prod(shape))
            base = (raw_a, raw_b)[which][0:rows, place[which]:place[which] + n]
            place[which] += n
            assert place[which] <= 8192
            names = " ".join("abc"[:len(shape)])
            view = base.rearrange(f"p ({names}) -> p {names}", **{"abc"[k]: shape[k] for k in range(len(shape))})
            raws.append((view, ap))
            return view, len(raws)

        def space(which, shape):
            n = int(np.prod(shape))
            base = (raw_a, raw_b)[which][:, place[which]:place[which] + n]
            place[which] += n
            assert place[which] <= 8192
            return base.rearrange("p (a b) -> p a b", a=shape[0])

        def bank(n):
            return (ps_ring + ps_s)[n % 4]

        def turn4(src, rows, width, dst, loaded):
            n = len(jobs)
            ps = bank(n)[0:width, 0:4 * rows].rearrange("p (k r) -> p k r", k=4)
            jobs.append((loaded, 0, [(ps[:, k, :], "turn", src(k), rows) for k in range(4)], [(dst, ps, 1.0)]))
            return n + 1

        def prep_l0(wq, wk, wv, wo, a, which):
            wqr, l1 = raw(which, wq.rearrange("(t p) d -> p t d", p=P), P, [8, D])
            wkr, l2 = raw(which, wk.rearrange("(t p) d -> p t d", p=P), P, [8, a.kw])
            wvr, l3 = raw(which, wv.rearrange("(t p) d -> p t d", p=P), P, [8, a.kw])
            wor, l4 = raw(which, wo, P, [8, P])
            wot = space(which, [8, P])
            dep = 0
            for c in range(2):
                dep = turn4(lambda k, c=c: wor[:, 4 * c + k, :], P, P, wot[:, 4 * c:4 * c + 4, :], l4)
            for c in range(4):
                ps = bank(len(jobs))[:, 0:4 * a.kw].rearrange("p (k r) -> p k r", k=4)
                mm = []
                for k in range(4):
                    h = 8 * (c // 2) + 2 * k + c % 2
                    rows = slice(64 * (h % 2), 64 * (h % 2) + 64)
                    mm.append((ps[:, k, :], "mm", wqr[rows, h // 2, :], wkr[rows, h // 2, :]))
                jobs.append((l4, 0, mm, [([w[:, 8 * (c // 2) + c % 2:8 * (c // 2) + 8:2, :] for w in fold_qk[a.name]], ps, 64 ** -0.5)]))
            for c in range(4):
                ps = bank(len(jobs))[0:a.kw, :].rearrange("p (k r) -> p k r", k=4)
                mm = []
                for k in range(4):
                    h = 8 * (c // 2) + 2 * k + c % 2
                    rows = slice(64 * (h % 2), 64 * (h % 2) + 64)
                    mm.append((ps[:, k, :], "mm", wvr[rows, h // 2, :], wot[rows, h // 2, :]))
                jobs.append((l4, dep, mm, [(fold_vo[a.name][0:a.kw, 8 * (c // 2) + c % 2:8 * (c // 2) + 8:2, :], ps, 1.0)]))

        def prep_last():
            wqr, l1 = raw(0, t["L1_xattn_Wq"], P, [8, P])
            wkr, l2 = raw(0, t["L1_xattn_Wk"], CD, [8, P])
            wvr, l3 = raw(0, t["L1_xattn_Wv"], CD, [8, P])
            wor, l4 = raw(1, t["L1_xattn_Wo"].rearrange("(t p) d -> p t d", p=P), P, [8, P])
            wgr, l5 = raw(1, t["L0_xattn_w_geglu"].rearrange("(t p) d -> p t d", p=P), P, [8, P])
            wfr, l6 = raw(1, t["L0_xattn_w_ffout"], P, [4, P])
            wqt, wkt = space(0, [8, P]), space(0, [8, CD])
            wvt = space(0, [8, CD])
            for c in range(2):
                for src, rows, dst in ((wqr, P, wqt), (wkr, CD, wkt), (wvr, CD, wvt)):
                    dep = turn4(lambda k, c=c, src=src: src[:, 4 * c + k, :], rows, P, dst[:, 4 * c:4 * c + 4, :], l6)
            for c in range(2):
                ps = bank(len(jobs))[:, 0:4 * CD].rearrange("p (k r) -> p k r", k=4)
                jobs.append((l6, dep, [(ps[:, k, :], "mm", wqt[:, 4 * c + k, :], wkt[:, 4 * c + k, :]) for k in range(4)],
                             [([w[:, 4 * c:4 * c + 4, :] for w in fold_qk["last"]], ps, 128 ** -0.5)]))
            for c in range(2):
                ps = bank(len(jobs))[0:CD, :].rearrange("p (k r) -> p k r", k=4)
                jobs.append((l6, dep, [(ps[:, k, :], "mm", wvt[:, 4 * c + k, :], wor[:, 4 * c + k, :]) for k in range(4)],
                             [(fold_vo["last"][0:CD, 4 * c:4 * c + 4, :], ps, 1.0)]))
            for c in range(2):
                turn4(lambda k, c=c: wgr[:, 4 * c + k, :], P, P, [w[:, 4 * c:4 * c + 4, :] for w in wg_t], l6)
            turn4(lambda k: wfr[:, k, :], P, P, wf_t[:, :, :], l6)

        prep_l0(t["L0_xattn_wq1"], t["L0_xattn_wk1"], t["L0_xattn_wv1"], t["L0_xattn_wo1"], SELF, 0)
        first_raws = len(raws)
        prep_l0(t["L0_xattn_wq2"], t["L0_xattn_wk2"], t["L0_xattn_wv2"], t["L0_xattn_wo2"], CROSS, 1)
        second_raws, second_jobs = len(raws), len(jobs)
        place[:] = [0, 0]
        prep_last()

        s_ident = sem("s_ident")
        s_raw = [sem(f"s_raw{i}") for i in range(3)]
        s_small = sem("s_small")
        s_x = [sem("s_x_first"), sem("s_x_rest")]
        prep_ready = sem("prep_ready")
        prep_copied = sem("prep_copied")
        prep_high = sem("prep_high")
        set_end = [first_raws, second_raws, len(raws)]
        set_sem = [0 if n < first_raws else 1 if n < second_raws else 2 for n in range(len(raws))]

        def raw_loaded(eng, n):
            k = set_sem[n - 1]
            eng.wait_ge(s_raw[k], 16 * (set_end[k] - (set_end[k - 1] if k else 0)))

        mask_h = sb("mask_h", [P, SEQ], I32)
        has_key = sb("has_key", [P, SEQ])
        any_key = sb("any_key", [P, 1])
        ones = sb("ones", [P, SEQ])
        key_sel = sb("key_sel", [P, 2, TILES])
        last_eps = sb("last_eps", [P, TILES])
        keys_spread = sem("keys_spread")
        s_ones_row = sem("s_ones_row")
        s_mask = sem("s_mask")
        s_bad = sem("s_bad")
        s_const = sem("s_const")

        phases = {}

        def phase_sems(name, names):
            phases[name] = {n: sem(f"{name}_{n}") for n in names}
            return phases[name]

        common = ["ring_done", "ring_high", "ring_free0", "ring_free1", "o_done", "o_copied", "back_done", "resid_done",
                  "rows_ready"]
        norm = ["stat", "var_ready", "scaled_ready", "rstd_ready", "norm_ready", "gain_done"]
        attn = ["scores_done", "max_done", "shifted", "exp_done", "sum_done", "recip_done", "prob_ready", "turned",
                "pt_high", "pt_copied", "krow_high", "krow_ready", "dup0", "dup1", "u_done", "u_copied"]
        ctx = ["crow0", "crow1"]
        sems = {"self": phase_sems("self", common + norm + attn), "cross": phase_sems("cross", common + norm + attn + ctx),
                "ffn": phase_sems("ffn", common + norm + ["up_done", "gate_done", "h_done"]),
                "last": phase_sems("last", common + attn + ctx + [
                    "mask0", "mask1", "mask_done", "out0", "out1", "scaled_ready", "fin_stat", "fin_var", "fin_rstd",
                    "fin_norm", "fin_gain", "fin_done"])}
        before = {"self": None, "cross": "self", "ffn": "cross", "last": "ffn"}

        def phase_begins(eng, name):
            if before[name]:
                eng.wait_ge(sems[before[name]]["resid_done"], NG)

        def ring_at(g, ring, k):
            n0 = ring * g.base + k
            uses = n0 // 2 if g.i is None else g.i * ring + n0 // 2
            return n0 % 2, uses

        block = stack.enter_context(nc.Block())

        @block.sync
        def _(sp):
            def load_set(k):
                lo = set_end[k - 1] if k else 0
                for view, ap in raws[lo:set_end[k]]:
                    dst = view
                    if len(ap.shape) == 2 and len(view.shape) == 3:
                        dst = view.rearrange("p a b -> p (a b)")
                    sp.dma_start(dst, ap).then_inc(s_raw[k], 16)

            xr = t["x"].rearrange("b s d -> (b s) d").rearrange("(t p) d -> p t d", p=P)
            cr = t["ctx_768"].rearrange("b s d -> (b s) d").rearrange("(t p) d -> p t d", p=P)
            orows = out.rearrange("b s d -> (b s) d").rearrange("(t p) d -> p t d", p=P)
            mr = t["mask_BxS2_if1"].rearrange("(a b) s -> a (b s)", a=1)
            first = 4 * TPG
            load_set(0)
            sp.dma_start(x[:, 0:first, :], xr[:, 0:first, :]).then_inc(s_x[0], 16)
            for n, src in (("ln1_g", "L0_xattn_ln1_g"), ("ln1_b", "L0_xattn_ln1_b"), ("ln2_g", "L0_xattn_ln2_g"),
                           ("ln2_b", "L0_xattn_ln2_b"), ("ln3_g", "L0_xattn_ln3_g"), ("ln3_b", "L0_xattn_ln3_b"),
                           ("gamma", "L1_xattn_gamma"), ("beta", "L1_xattn_beta")):
                sp.dma_start(gains[n][:], t[src].rearrange("(a d) -> a d", a=1).to_broadcast([P, D])).then_inc(s_small, 16)
            for c, n in enumerate(("L0_xattn_bo1", "L0_xattn_bo2", "L0_xattn_b_ffout")):
                sp.dma_start(cols[:, c:c + 1], t[n].rearrange("(d a) -> d a", a=1)).then_inc(s_small, 16)
            for c in range(8):
                sp.dma_start(cols[:, 3 + c:4 + c], t["L0_xattn_b_geglu"][c * P:(c + 1) * P].rearrange("(d a) -> d a", a=1)).then_inc(s_small, 16)
            load_set(1)
            sp.dma_start(x[:, first:TILES, :], xr[:, first:TILES, :]).then_inc(s_x[1], 16)
            sp.dma_start(mask_h[:], t["mask_BxS2_if1"]).then_inc(s_mask, 16)
            sp.wait_ge(prep_ready, second_jobs)
            load_set(2)

            for a in (SELF, CROSS, LAST):
                s = sems[a.name]
                phase_begins(sp, a.name)

                def body(g):
                    nxt, dup, og = g.plus(2), g.plus(1), g.plus(-2)

                    def known(v):
                        return v if isinstance(v, int) else sp.snap(v)

                    dup_reads = known(dup.at(1, 1))
                    if a.ctx:
                        tile, turned, copied = known(nxt.at(TPG)), known(g.at(a.ring, 1)), known(g.half(128, 128))
                    if a.mask:
                        token, masked = known(nxt.at(TOK)), known(g.at(1, 1))
                        otile, finished = known(og.at(TPG)), known(og.at(1, 1))

                    if nxt and a.ctx:
                        if g:
                            if g.i is None:
                                sp.wait_ge(s["ring_done"], turned)
                            sp.wait_ge(s[f"dup{g.par}"], copied)
                        sp.dma_start(crow[:, g.par, :, :], cr[:, bass.ds(tile, TPG), :]).then_inc(s[f"crow{g.par}"], 16)
                    if nxt and a.mask:
                        if g:
                            sp.wait_ge(s["mask_done"], masked)
                        sp.dma_start(mask_i[96:97, g.par, :], mr[:, bass.ds(token, TOK)]).then_inc(s[f"mask{g.par}"], 16)
                    if dup:
                        sp.wait_ge(s["krow_ready"], dup_reads)
                        for part in range(2):
                            for r in range(2):
                                for b2 in range(2):
                                    sp.dma_start(
                                        cdup[part][64 * r:64 * r + 64, dup.par, :, 0:a.kw].rearrange(
                                            "p (t b) e -> p t b e", b=2)[:, :, b2, :].bitcast(F32),
                                        krow[part][64 * b2:64 * b2 + 64, dup.par, :, 0:a.kw].bitcast(F32)).then_inc(s[f"dup{dup.par}"], 16)
                    if og and a.mask:
                        sp.wait_ge(s["fin_done"], finished)
                        sp.dma_start(orows[:, bass.ds(otile, TPG), :], orow[:, og.par, :, :]).then_inc(s[f"out{og.par}"], 16)
                over_groups(sp, body)
            for p in range(2):
                sp.wait_ge(sems["last"][f"out{p}"], 16 * (NG // 2))

        @block.tensor
        def _(pe):
            pe.wait_ge(s_ident, 2)
            for n, (loaded, dep, mm, _) in enumerate(jobs):
                raw_loaded(pe, loaded)
                wait(pe, prep_copied, max(n - 3, dep))
                for o, kind, a, b in mm:
                    if kind == "turn":
                        last = pe.transpose(o, a, ident[0:b, 0:b])
                    else:
                        last = pe.matmul(o, a, b, start=True, stop=True)
                last.then_inc(prep_ready, 1)
            pe.wait_ge(s_bad, 5)
            for b2 in range(2):
                last = pe.matmul(ps_pt[64 * b2:64 * b2 + 64, 0:TILES], ones[:], key_sel[:, b2, :], start=True, stop=True)
            last.then_inc(keys_spread, 1)
            pe.wait_ge(s_bad, 6)
            pe.wait_ge(prep_copied, len(jobs))

            def turn_back(s, g, ps_o=ps_o):
                pe.wait_ge(s["o_copied"], g.at(1, 1))
                for k in range(TPG):
                    last = pe.transpose(ps_o[:, TOK + k * P:TOK + (k + 1) * P], ot[:, k * P:(k + 1) * P], ident[:, :])
                last.then_inc(s["back_done"], 1)

            def head_bank(s, g, ring, a):
                bank_, uses = ring_at(g, ring, 0)
                wait(pe, s[f"ring_free{bank_}"], uses)
                pe.wait_ge(s["rows_ready"], g.at(1, 1))
                for k in range(TPG):
                    last = pe.transpose(ps_ring[bank_][:, k * P:(k + 1) * P], xrow[:, g.par, k, :], ident[:, :])
                if a is not None and a.ctx:
                    pe.wait_ge(s[f"crow{g.par}"], g.half(16, 16))
                    for k in range(TPG):
                        last = pe.transpose(ps_ring[bank_][0:CD, TOK + k * P:TOK + (k + 1) * P], crow[:, g.par, k, :], ident[:, :])
                last.then_inc(s["ring_done"], 1)

            def attention(a):
                s = sems[a.name]
                wqk, wvo = fold_qk[a.name], fold_vo[a.name]
                per_step = a.pairs // 2

                def scores(g, b):
                    if b == 0:
                        for k in (a.pairs - 1, a.pairs):
                            bank_, uses = ring_at(g, a.ring, k)
                            pe.wait_ge(s[f"ring_free{bank_}"], uses + 1)
                        if a.mask:
                            pe.wait_ge(s["mask_done"], g.at(1, 1))
                            if g.i is None and g.base == 0:
                                pe.wait_ge(s_ones_row, 1)
                    wait(pe, s["shifted"], g.at(BPG, b - 1))
                    for q in range(a.pairs):
                        last = pe.matmul(ps_s[b % 2][:, q * SEQ:(q + 1) * SEQ],
                                         yt[0:a.srows, g.par, b, q * P:(q + 1) * P],
                                         kt[0:a.srows, g.par, b * SEQ:(b + 1) * SEQ], start=True, stop=True)
                    last.then_inc(s["scores_done"], 1)

                def queries(g, k):
                    bank_, uses = ring_at(g, a.ring, k + 1)
                    wait(pe, s[f"ring_free{bank_}"], uses)
                    if k == 0:
                        hb, huses = ring_at(g, a.ring, 0)
                        pe.wait_ge(s[f"ring_free{hb}"], huses + 1)
                    for j in range(2):
                        last = matmul3(pe, ps_ring[bank_][0:a.kw, j * TOK:(j + 1) * TOK],
                                       [w[:, 2 * k + j, :] for w in wqk], [v[:, g.par, :] for v in xt])
                    last.then_inc(s["ring_done"], 1)

                def turn_probs(g, b):
                    pe.wait_ge(s["prob_ready"], g.at(BPG, b + 1))
                    wait(pe, s["pt_copied"], g.at(BPG, b))
                    for k in range(a.turns):
                        last = pe.transpose(ps_pt[:, k * P:(k + 1) * P], prob[:, b, k * P:(k + 1) * P], ident[:, :])
                    last.then_inc(s["turned"], 1)

                def mix(g, b, r):
                    if r == 0:
                        pe.wait_ge(s["pt_copied"], g.at(BPG, b + 1))
                        if b == 0:
                            pe.wait_ge(s[f"dup{g.par}"], g.half(128, 128))
                    wait(pe, s["u_copied"], g.at(2 * BPG, 2 * b + r - 1))
                    for part in (1, 0):
                        last = pe.matmul(ps_u[r][0:a.kw, 0:a.turns * P], cdup[part][:, g.par, b, 0:a.kw],
                                         pt[r][:, b % 2, 0:a.turns * P], start=(part == 1), stop=(part == 0))
                    last.then_inc(s["u_done"], 1)

                def project(g, part):
                    if part == 0:
                        pe.wait_ge(s["u_copied"], g.at(2 * BPG, 2 * BPG))
                        wait(pe, s["resid_done"], g.at(1))
                    half = a.heads // 2
                    for h in range(part * half, part * half + half):
                        last = pe.matmul(ps_o[:, 0:TOK], wvo[0:a.kw, h, :], ut[0:a.kw, g.par, h, :],
                                         start=(h == 0), stop=(h == a.heads - 1))
                    if part == 1:
                        last.then_inc(s["o_done"], 1)

                def body(g):
                    for b in range(BPG):
                        if g:
                            scores(g, b)
                        fill = list(range((b - 1) * per_step, b * per_step)) if b in (1, 2) and g.plus(1) else []
                        while len(fill) > 2 or len(fill) == 2 and per_step == 2:
                            queries(g.plus(1), fill.pop(0))
                        tg, tb = back(g, b, 2)
                        if tg:
                            turn_probs(tg, tb)
                        if b == 0 and g.plus(-2):
                            project(g.plus(-2), 1)
                        if b == BPG - 1 and g.plus(-1):
                            project(g.plus(-1), 0)
                        ug, ub = back(g, b, 3)
                        for r in range(2):
                            if fill:
                                queries(g.plus(1), fill.pop(0))
                            if ug:
                                mix(ug, ub, r)
                        if b == 1 and g.plus(-2):
                            turn_back(s, g.plus(-2))
                        if b == BPG - 1 and g.plus(2):
                            head_bank(s, g.plus(2), a.ring, a)
                over_groups(pe, body)

            def ffn():
                s = sems["ffn"]

                def up(g):
                    hb, huses = ring_at(g, 1, 0)
                    pe.wait_ge(s[f"ring_free{hb}"], huses + 1)
                    for c in range(4):
                        dst = (ps_s[0], ps_s[1], ps_u[0], ps_u[1])[c]
                        wait(pe, s["h_done"], g.at(4, c - 3))
                        v = [v[:, g.par, :] for v in xt]
                        matmul3(pe, dst[:, 0:TOK], [w[:, 4 + c, :] for w in wg_t], v)
                        matmul3(pe, dst[:, TOK:2 * TOK], [w[:, c, :] for w in wg_t], v).then_inc(s["up_done"], 1)

                def down(g):
                    pe.wait_ge(s["h_done"], g.at(4, 4))
                    wait(pe, s["resid_done"], g.at(1, -1))
                    for c in range(4):
                        last = pe.matmul(ps_down[g.par][:, 0:TOK], wf_t[:, c, :], ut[:, g.par, c, :], start=(c == 0), stop=(c == 3))
                    last.then_inc(s["o_done"], 1)

                def body(g):
                    if g.plus(-1):
                        down(g.plus(-1))
                    if g.plus(1):
                        up(g.plus(1))
                    if g.plus(2):
                        head_bank(s, g.plus(2), 1, None)
                    if g.plus(-1):
                        turn_back(s, g.plus(-1), ps_down[g.plus(-1).par])
                over_groups(pe, body, lead=3)

            for name, run in (("self", lambda: attention(SELF)), ("cross", lambda: attention(CROSS)),
                              ("ffn", ffn), ("last", lambda: attention(LAST))):
                phase_begins(pe, name)
                run()

        def ring_out(eng, copy, s, g, a, k):
            bank_, uses = ring_at(g, a.ring, k)
            eng.wait_ge(s["ring_done"], g.at(a.ring, k + 1))
            copy(yt[0:a.kw, g.par, :, (2 * k - 2) * SEQ:2 * k * SEQ].rearrange("p b (h i) -> p b h i", h=2),
                 ps_ring[bank_][0:a.kw, :].rearrange("p (h b i) -> p b h i", h=2, b=BPG)).then_inc(s[f"ring_free{bank_}"], 1)

        def ring_step(eng, copy, s, g, b, a, which):
            per_step = a.pairs // 2
            if b in (1, 2) and g.plus(1):
                for k in which:
                    if k < per_step:
                        ring_out(eng, copy, s, g.plus(1), a, (b - 1) * per_step + 1 + k)

        def head_ring(a):
            return a.ring if a else 1

        @block.scalar
        def _(act):
            def copy(dst, src):
                return act.activation(dst, src, ACT.Copy)

            def head_high(s, g, a):
                if not g:
                    return
                bank_, uses = ring_at(g, head_ring(a), 0)
                act.wait_ge(s["ring_done"], g.at(head_ring(a), 1))
                ps = ps_ring[bank_]
                ins = copy(xt[0][:, g.par, :], ps[:, 0:TOK])
                if a:
                    ins = copy(kt[0:a.kw, g.par, :], ps[0:a.kw, TOK:2 * TOK] if a.ctx else ps[:, 0:TOK])
                ins.then_inc(s["ring_high"], 1)

            def o_out(s, g, bias, ps_o=ps_o):
                act.wait_ge(s["o_done"], g.at(1, 1))
                wait(act, s["back_done"], g.at(1))
                if bias is None:
                    ins = copy(ot[:], ps_o[:, 0:TOK])
                else:
                    ins = act.activation(ot[:], ps_o[:, 0:TOK], ACT.Identity, bias=bias)
                ins.then_inc(s["o_copied"], 1)

            for n, (_, _, _, outs) in enumerate(jobs):
                (dst, src, scale), = outs
                if isinstance(dst, list):
                    act.wait_ge(prep_ready, n + 1)
                    wait(act, prep_copied, n)
                    act.activation(dst[0], src, ACT.Copy, scale=scale).then_inc(prep_high, 1)
                elif n % 2:
                    act.wait_ge(prep_ready, n + 1)
                    act.wait_ge(prep_copied, n)
                    act.activation(dst, src, ACT.Copy, scale=scale).then_inc(prep_copied, 1)
            act.wait_ge(s_small, 16 * 19)

            def attention(a, bias):
                s = sems[a.name]

                def body(g):
                    for b in range(BPG):
                        ring_step(act, copy, s, g, b, a, [0])
                        if g:
                            act.wait_ge(s["shifted"], g.at(BPG, b + 1))
                            act.activation(prob[:, b, 0:a.pairs * SEQ], prob[:, b, 0:a.pairs * SEQ], ACT.Exp)\
                               .then_inc(s["exp_done"], 1)
                        if b == 0:
                            head_high(s, g.plus(1), a)
                        tg, tb = back(g, b, 2)
                        if tg:
                            act.wait_ge(s["turned"], tg.at(BPG, tb + 1))
                            for r in range(2):
                                half = slice(64 * r, 64 * r + 64)
                                copy(pt[r][half, tb % 2, 0:a.turns * P], ps_pt[half, 0:a.turns * P]).then_inc(s["pt_high"], 1)
                        ug, ub = back(g, b, 3)
                        for r in range(2):
                            ring_step(act, copy, s, g, b, a, [2 + r] if a.heads == 16 else [1] if r == 0 else [])
                            if ug:
                                act.wait_ge(s["u_done"], ug.at(2 * BPG, 2 * ub + r + 1))
                                if ub == 0 and r == 0:
                                    wait(act, s["o_done"], ug.at(1, -1))
                                copy(ut[0:a.kw, ug.par, 0:a.heads, ub * SEQ:(ub + 1) * SEQ].rearrange(
                                        "e (t r k) i -> e t r k i", r=2, k=2)[:, :, r, :, :],
                                     ps_u[r][0:a.kw, 0:a.turns * P].rearrange("e (t k i) -> e t k i", k=2, i=SEQ))\
                                    .then_inc(s["u_copied"], 1)
                        if b == 0 and g.plus(-2):
                            o_out(s, g.plus(-2), bias)
                over_groups(act, body)

            def ffn():
                s = sems["ffn"]

                def body(g):
                    if g.plus(-1):
                        o_out(s, g.plus(-1), cols[:, 2:3], ps_down[g.plus(-1).par])
                    if g.plus(1):
                        n = g.plus(1)
                        for c in range(4):
                            act.wait_ge(s["up_done"], n.at(4, c + 1))
                            wait(act, s["h_done"], n.at(4, c - 3))
                            act.activation(yt[:, 0, c, 0:TOK], (ps_s[0], ps_s[1], ps_u[0], ps_u[1])[c][:, 0:TOK],
                                           ACT.Gelu, bias=cols[:, 7 + c:8 + c]).then_inc(s["gate_done"], 1)
                    head_high(s, g.plus(2), None)
                over_groups(act, body, lead=3)

            for name, run in (("self", lambda: attention(SELF, cols[:, 0:1])), ("cross", lambda: attention(CROSS, cols[:, 1:2])),
                              ("ffn", ffn), ("last", lambda: attention(LAST, None))):
                phase_begins(act, name)
                run()

        @block.vector
        def _(dve):
            def copy(dst, src):
                return dve.tensor_copy(dst, src)

            def low(dst, whole, high):
                return dve.tensor_tensor(dst, whole, high, ALU.subtract)

            def head_low(s, g, a):
                if not g:
                    return
                bank_, uses = ring_at(g, head_ring(a), 0)
                dve.wait_ge(s["ring_high"], g.at(1, 1))
                low(xt[1][:, g.par, :], ps_ring[bank_][:, 0:TOK], xt[0][:, g.par, :]).then_inc(s[f"ring_free{bank_}"], 1)

            dve.memset(mhalf[:], -0.5).then_inc(s_const, 1)
            dve.memset(eps[:], EPS).then_inc(s_const, 1)
            dve.memset(zero[:], 0.0).then_inc(s_const, 1)
            split = 0
            for n, (_, _, _, outs) in enumerate(jobs):
                (dst, src, scale), = outs
                if isinstance(dst, list):
                    split += 1
                    dve.wait_ge(prep_high, split)
                    dve.scalar_tensor_tensor(out=dst[1], in0=src, scalar=scale, in1=dst[0], op0=ALU.mult,
                                             op1=ALU.subtract).then_inc(prep_copied, 1)
                elif n % 2 == 0:
                    dve.wait_ge(prep_ready, n + 1)
                    wait(dve, prep_copied, n)
                    dve.tensor_scalar(dst, src, scale, None, ALU.mult).then_inc(prep_copied, 1)
            dve.wait_ge(s_mask, 16)
            dve.tensor_scalar(has_key[:], mask_h[:], 0.0, None, ALU.not_equal).then_inc(s_bad, 1)
            dve.wait_ge(s_bad, 1)
            dve.tensor_reduce(any_key[:], has_key[:], AX_X, ALU.max).then_inc(s_bad, 1)
            dve.memset(ones[:], 1.0).then_inc(s_bad, 1)
            dve.wait_ge(s_bad, 3)
            dve.wait_ge(s_ident, 2)
            for b2 in range(2):
                dve.tensor_scalar(key_sel[:, b2, :], ident[:, b2:P:2], any_key[:, 0:1], None, ALU.mult).then_inc(s_bad, 1)
            dve.wait_ge(keys_spread, 1)
            dve.tensor_scalar(last_eps[:], ps_pt[:, 0:TILES], 0.0, -3e38, ALU.is_equal, ALU.mult).then_inc(s_bad, 1)
            dve.wait_ge(s_bad, 6)
            dve.tensor_scalar(row_eps[:], last_eps[:], 10.0, None, ALU.mult).then_inc(s_bad, 1)
            dve.wait_ge(s_bad, 7)
            dve.tensor_tensor(last_eps[:], row_eps[:], row_eps[:], ALU.subtract).then_inc(s_bad, 1)
            dve.wait_ge(s_bad, 8)
            dve.tensor_scalar(row_eps[:], last_eps[:], EPS, None, ALU.add).then_inc(s_bad, 1)
            dve.wait_ge(s_x[0], 16)
            dve.wait_ge(s_small, 16 * 19)

            def norm_stats(s, g, src, stat, var):
                for k in range(TPG):
                    dve.bn_stats(stats[:, k, :], src(k)).then_inc(s[stat], 1)
                dve.wait_ge(s[stat], g.at(TPG + 1, TPG))
                dve.memset(carrier[:], 0.0).then_inc(s[stat], 1)
                for k in range(TPG):
                    ins = dve.bn_aggr(moments[:, k, :], stats[:, k, :])
                ins.then_inc(s[var], 1)

            def norm_rows(s, g, src, dst, rst, done):
                dve.wait_ge(s[rst], g.at(1, 1))
                for k in range(TPG):
                    ins = dve.tensor_scalar(dst(k), src(k), moments[:, k, 0:1], rstd[:, k:k + 1], ALU.subtract, ALU.mult)
                ins.then_inc(s[done], 1)

            def ln_stats(s, g):
                norm_stats(s, g, lambda k: x[:, bass.ds(g.at(TPG, k), 1), :].rearrange("p a d -> p (a d)"), "stat", "var_ready")

            def ln_rows(s, g, ring, dup):
                if g.i is not None or g.base >= 2:
                    dve.wait_ge(s["ring_done"], g.at(ring, 1 - 2 * ring))
                    if dup:
                        dve.wait_ge(s["krow_ready"], g.at(1, -1))
                norm_rows(s, g, lambda k: x[:, bass.ds(g.at(TPG, k), 1), :].rearrange("p a d -> p (a d)"),
                          lambda k: xrow[:, g.par, k, :], "rstd_ready", "norm_ready")

            def residual(s, g, ps_o=ps_o):
                dve.wait_ge(s["back_done"], g.at(1, 1))
                xs = x[:, bass.ds(g.at(TPG), TPG), :].rearrange("p t d -> p (t d)")
                dve.tensor_tensor(xs, ps_o[:, TOK:2 * TOK], xs, ALU.add).then_inc(s["resid_done"], 1)

            def final_rows(s, g):
                dve.wait_ge(s["back_done"], g.at(1, 1))
                if g.i is not None or g.base >= 2:
                    dve.wait_ge(s[f"out{g.par}"], g.half(16))
                o = orow[:, g.par, :, :].rearrange("p t d -> p (t d)")
                xs = x[:, bass.ds(g.at(TPG), TPG), :].rearrange("p t d -> p (t d)")
                dve.tensor_tensor(o, ps_o[:, TOK:2 * TOK], xs, ALU.add).then_inc(s["resid_done"], 1)
                dve.wait_ge(s["resid_done"], g.at(1, 1))
                norm_stats(s, g, lambda k: orow[:, g.par, k, :], "fin_stat", "fin_var")

            def final_norm(s, g):
                norm_rows(s, g, lambda k: orow[:, g.par, k, :], lambda k: orow[:, g.par, k, :], "fin_rstd", "fin_norm")

            def attention(a):
                s = sems[a.name]
                n = a.pairs * SEQ

                def body(g):
                    for b in range(BPG):
                        tg, tb = back(g, b, 3)
                        if tg:
                            dve.wait_ge(s["pt_high"], tg.at(2 * BPG, 2 * tb + 2))
                            for r in range(2):
                                half, other = slice(64 * r, 64 * r + 64), slice(64 - 64 * r, 128 - 64 * r)
                                ins = low(pt[r][other, tb % 2, 0:a.turns * P], ps_pt[half, 0:a.turns * P],
                                          pt[r][half, tb % 2, 0:a.turns * P])
                            ins.then_inc(s["pt_copied"], 1)
                        if g:
                            pb = prob[:, b, 0:n].rearrange("p (q j) -> p q j", j=SEQ)
                            ps = ps_s[b % 2][:, 0:n].rearrange("p (q j) -> p q j", j=SEQ)
                            dve.wait_ge(s["scores_done"], g.at(BPG, b + 1))
                            dve.tensor_reduce(smax[:, b, 0:a.pairs], ps, AX_X, ALU.max).then_inc(s["max_done"], 1)
                            dve.wait_ge(s["max_done"], g.at(BPG, b + 1))
                            wait(dve, s["turned"], g.at(BPG, b - 3))
                            dve.tensor_tensor(pb, ps, smax[:, b, 0:a.pairs].unsqueeze(2).to_broadcast([P, a.pairs, SEQ]),
                                              ALU.subtract).then_inc(s["shifted"], 1)
                        if a.heads == 16:
                            ring_step(dve, copy, s, g, b, a, [1])
                        if b == 2 and g.plus(-2):
                            if a.mask:
                                final_rows(s, g.plus(-2))
                            else:
                                residual(s, g.plus(-2))
                        if b == 3 and g.plus(-2) and a.mask:
                            final_norm(s, g.plus(-2))
                        if g:
                            dve.wait_ge(s["exp_done"], g.at(BPG, b + 1))
                            dve.tensor_reduce(ssum[:, b, 0:a.pairs], pb, AX_X, ALU.add).then_inc(s["sum_done"], 1)
                            dve.wait_ge(s["sum_done"], g.at(BPG, b + 1))
                            dve.reciprocal(srec[:, b, 0:a.pairs], ssum[:, b, 0:a.pairs]).then_inc(s["recip_done"], 1)
                        if b == 0:
                            head_low(s, g.plus(1), a)
                        if b == 0 and g.plus(2) and a.ln:
                            ln_stats(s, g.plus(2))
                        if b == 1 and g.plus(2) and a.ln:
                            ln_rows(s, g.plus(2), a.ring, not a.ctx)
                    nxt = g.plus(2)
                    if nxt and a.mask:
                        dve.wait_ge(s[f"mask{nxt.par}"], nxt.half(16, 16))
                        if g:
                            dve.wait_ge(s["scores_done"], g.at(BPG, BPG))
                        dve.tensor_scalar(kt[96:97, g.par, :], mask_i[96:97, g.par, :], 0.0, MASKED,
                                          ALU.is_equal, ALU.mult).then_inc(s["mask_done"], 1)
                over_groups(dve, body, before_loop=(lambda: dve.wait_ge(s_x[1], 16)) if a is SELF else None)

            def ffn():
                s = sems["ffn"]

                def body(g):
                    if g.plus(-2):
                        residual(s, g.plus(-2), ps_down[g.par])
                    if g.plus(3):
                        ln_stats(s, g.plus(3))
                    for c in range(4):
                        if c == 2 and g.plus(3):
                            ln_rows(s, g.plus(3), 1, False)
                        if g.plus(1):
                            n = g.plus(1)
                            dve.wait_ge(s["gate_done"], n.at(4, c + 1))
                            if c == 0:
                                wait(dve, s["o_done"], n.at(1, -1))
                            dve.scalar_tensor_tensor(out=ut[:, n.par, c, :], in0=(ps_s[0], ps_s[1], ps_u[0], ps_u[1])[c][:, TOK:2 * TOK],
                                                     scalar=cols[:, 3 + c:4 + c], in1=yt[:, 0, c, 0:TOK],
                                                     op0=ALU.add, op1=ALU.mult).then_inc(s["h_done"], 1)
                    head_low(s, g.plus(2), None)
                over_groups(dve, body, lead=3)

            for name, run in (("self", lambda: attention(SELF)), ("cross", lambda: attention(CROSS)),
                              ("ffn", ffn), ("last", lambda: attention(LAST))):
                phase_begins(dve, name)
                run()

        @block.gpsimd
        def _(pool):
            pool.memset(ident[:], 0.0).then_inc(s_ident, 1)
            pool.wait_ge(s_ident, 1)
            pool.affine_select(out=ident[:], in_=ident[:], compare_op=ALU.not_equal, fill=1.0, base=0,
                               pattern=[[-1, P]], channel_multiplier=1).then_inc(s_ident, 1)
            pool.wait_ge(s_const, 3)
            pool.wait_ge(s_small, 16 * 19)
            pool.wait_ge(s_bad, 9)

            def root(s, g, var, scaled, rst, row_eps=None):
                pool.wait_ge(s[var], g.at(1, 1))
                e = eps[:] if row_eps is None else row_eps[:, bass.ds(g.at(TPG), TPG)]
                pool.tensor_tensor(varp[:], moments[:, :, 1], e, ALU.add).then_inc(s[scaled], 1)
                pool.wait_ge(s[scaled], g.at(1, 1))
                pool.tensor_tensor(rstd[:], varp[:], mhalf[:], ALU.pow).then_inc(s[rst], 1)

            def affine(s, g, rows, gain, bias, norm, gained, done):
                pool.wait_ge(s[norm], g.at(1, 1))
                pool.tensor_tensor(rows, rows, gain[:].unsqueeze(1).to_broadcast([P, TPG, D]), ALU.mult).then_inc(s[gained], 1)
                pool.wait_ge(s[gained], g.at(1, 1))
                pool.tensor_tensor(rows, rows, bias[:].unsqueeze(1).to_broadcast([P, TPG, D]), ALU.add).then_inc(s[done], 1)

            def attention(a, gain, bias):
                s = sems[a.name]
                n = a.pairs * SEQ
                if a.mask:
                    pool.memset(yt[96:97, :, :, :], 1.0).then_inc(s_ones_row, 1)
                    pool.wait_ge(s_ones_row, 1)

                def body(g):
                    nxt = g.plus(2)
                    for b in range(BPG):
                        if g:
                            pool.wait_ge(s["recip_done"], g.at(BPG, b + 1))
                            pb = prob[:, b, 0:n].rearrange("p (q j) -> p q j", j=SEQ)
                            pool.tensor_tensor(pb, pb, srec[:, b, 0:a.pairs].unsqueeze(2).to_broadcast([P, a.pairs, SEQ]),
                                               ALU.mult).then_inc(s["prob_ready"], 1)
                        if a.mask and g.plus(-2):
                            og = g.plus(-2)
                            if b == 2:
                                root(s, og, "fin_var", "scaled_ready", "fin_rstd", row_eps)
                            if b == 3:
                                affine(s, og, orow[:, og.par, :, :], gain, bias, "fin_norm", "fin_gain", "fin_done")
                        if nxt and a.ln and b == 0:
                            root(s, nxt, "var_ready", "scaled_ready", "rstd_ready")
                        if nxt and a.ln and b == 1:
                            affine(s, nxt, xrow[:, g.par, :, :], gain, bias, "norm_ready", "gain_done", "rows_ready")
                        if nxt and not a.ln and b == 1:
                            if g:
                                pool.wait_ge(s["ring_done"], g.at(a.ring, 1))
                            pool.tensor_copy(xrow[:, g.par, :, :], x[:, bass.ds(nxt.at(TPG), TPG), :]).then_inc(s["rows_ready"], 1)
                    kg = g.plus(1)
                    if kg:
                        rows = (crow if a.ctx else xrow)[:, kg.par, :, 0:a.kw]
                        if a.ctx:
                            pool.wait_ge(s[f"crow{kg.par}"], kg.half(16, 16))
                        if kg.i is not None or kg.base >= 2:
                            pool.wait_ge(s[f"dup{kg.par}"], kg.half(128))
                            pool.wait_ge(s["u_done"], kg.at(2 * BPG, -2 * BPG))
                        hi, lo = (k[:, kg.par, :, 0:a.kw] for k in krow)
                        pool.tensor_tensor(hi, rows, zero[:, 0:1].unsqueeze(2).to_broadcast([P, TPG, a.kw]), ALU.add)\
                            .then_inc(s["krow_high"], 1)
                        pool.wait_ge(s["krow_high"], kg.at(1, 1))
                        pool.tensor_tensor(lo, rows, hi, ALU.subtract).then_inc(s["krow_ready"], 1)
                over_groups(pool, body)

            def ffn():
                s = sems["ffn"]

                def body(g):
                    n = g.plus(3)
                    if n:
                        root(s, n, "var_ready", "scaled_ready", "rstd_ready")
                        affine(s, n, xrow[:, n.par, :, :], gains["ln3_g"], gains["ln3_b"], "norm_ready", "gain_done", "rows_ready")
                over_groups(pool, body, lead=3)

            for name, run in (("self", lambda: attention(SELF, gains["ln1_g"], gains["ln1_b"])),
                              ("cross", lambda: attention(CROSS, gains["ln2_g"], gains["ln2_b"])),
                              ("ffn", ffn), ("last", lambda: attention(LAST, gains["gamma"], gains["beta"]))):
                phase_begins(pool, name)
                run()


INPUTS = ["x", "ctx_768", "mask_BxS2_if1", "L0_xattn_wq1", "L0_xattn_wk1", "L0_xattn_wv1", "L0_xattn_wo1", "L0_xattn_bo1",
          "L0_xattn_wq2", "L0_xattn_wk2", "L0_xattn_wv2", "L0_xattn_wo2", "L0_xattn_bo2", "L0_xattn_w_geglu",
          "L0_xattn_b_geglu", "L0_xattn_w_ffout", "L0_xattn_b_ffout", "L0_xattn_ln1_g", "L0_xattn_ln1_b",
          "L0_xattn_ln2_g", "L0_xattn_ln2_b", "L0_xattn_ln3_g", "L0_xattn_ln3_b", "L1_xattn_Wq", "L1_xattn_Wk",
          "L1_xattn_Wv", "L1_xattn_Wo", "L1_xattn_gamma", "L1_xattn_beta"]


def kernel(**inputs):
    import numpy as _np
    import concourse.bacc as _bacc
    from concourse import mybir as _mybir
    from concourse.bass_utils import run_bass_kernel_spmd as _run

    nc = _bacc.Bacc("TRN2", target_bir_lowering=False, num_devices=1)
    arrays, handles = {}, {}
    for name in INPUTS:
        a = _np.ascontiguousarray(inputs[name])
        arrays[f"in_{name}"] = a
        handles[name] = nc.dram_tensor(f"in_{name}", a.shape, _mybir.dt.from_np(a.dtype), kind="ExternalInput").ap()
    out = nc.dram_tensor("out_rows", (NB, SEQ, D), F32, kind="ExternalOutput").ap()
    build(nc, handles, out)
    r = _run(nc, [arrays], core_ids=[0])
    return r.results[0]["out_rows"]
```

```python
from contextlib import ExitStack

import numpy as np
import concourse.bass as bass
from concourse import mybir
from concourse.alu_op_type import AluOpType as ALU

F32 = mybir.dt.float32
F32R = mybir.dt.float32r
I32 = mybir.dt.int32
ACT = mybir.ActivationFunctionType
AX_X = mybir.AxisListType.X

P = 128
NB, SEQ, D = 128, 64, 128
CD = 96
BPG = 4
TOK = BPG * SEQ
TPG = TOK // P
NG = NB // BPG
TILES = NB * SEQ // P
FF = 4 * D
SMALL = 4 + 3 + 8
EPS = 1e-5
MASKED = -1e30


class Group:

    def __init__(self, base, i=None):
        self.base, self.i, self.par = base, i, base % 2

    def at(self, mult, add=0):
        c = mult * self.base + add
        return c if self.i is None else self.i * (2 * mult) + c

    def half(self, mult, add=0):
        c = mult * (self.base // 2) + add
        return c if self.i is None else self.i * mult + c

    def plus(self, n):
        return Group(self.base + n, self.i)

    def __bool__(self):
        return self.i is not None or 0 <= self.base < NG


def over_groups(eng, body, lead=2, before_loop=None):
    end = (NG - lead) // 2 * 2
    for g in range(-lead, 2):
        body(Group(g))
    if before_loop:
        before_loop()
    with eng.Fori(0, (end - 2) // 2) as i:
        body(Group(2, i))
        body(Group(3, i))
    for g in range(end, NG + 2):
        body(Group(g))


def back(g, b, n):
    return (g, b - n) if b >= n else (g.plus(-1), b - n + BPG)


def matmul3(pe, out, w, v, start=True, stop=True):
    (w_hi, w_lo), (v_hi, v_lo) = w, v
    pe.matmul(out, w_lo, v_hi, start=start, stop=False)
    pe.matmul(out, w_hi, v_lo, start=False, stop=False)
    return pe.matmul(out, w_hi, v_hi, start=False, stop=stop)


def wait(eng, sem, value):
    if not isinstance(value, int) or value > 0:
        eng.wait_ge(sem, value)


class Attn:

    def __init__(self, name, heads, kw, ctx, ln, mask):
        self.name, self.heads, self.kw, self.ctx, self.ln, self.mask = name, heads, kw, ctx, ln, mask
        self.pairs = heads // 2
        self.turns = heads // 4
        self.ring = heads // 2 + 1
        self.narrow = heads == 16
        self.fills = ([], [0, 1, 2, 3], [4, 5], [6, 7]) if self.narrow else ([], [0, 1], [2], [3])
        self.qrows = P if self.narrow else kw


SELF = Attn("self", 16, D, ctx=False, ln=True, mask=False)
CROSS = Attn("cross", 16, CD, ctx=True, ln=True, mask=False)
LAST = Attn("last", 8, CD, ctx=True, ln=False, mask=True)


def build(nc, t, out):
    with ExitStack() as stack:
        def sb(name, shape, dt=F32):
            return stack.enter_context(nc.sbuf_tensor(name, shape, dt))

        def sem(name):
            return stack.enter_context(nc.semaphore(name))

        ps_scores = stack.enter_context(nc.psum_tensor("ps_scores", [P, 2, 512], F32))
        ps_s = [ps_scores[:, i, :] for i in range(2)]
        ps_ring = [stack.enter_context(nc.psum_tensor(f"ps_ring{i}", [P, 512], F32)) for i in range(2)]
        ps_v = [stack.enter_context(nc.psum_tensor(f"ps_v{i}", [P, 512], F32)) for i in range(2)]
        ps_pt = stack.enter_context(nc.psum_tensor("ps_pt", [P, 512], F32))
        ps_o = stack.enter_context(nc.psum_tensor("ps_o", [P, 512], F32))

        ps_down = [ps_o, ps_pt]

        x = sb("x_rows", [P, TILES, D])
        ident = sb("ident", [P, P])
        yt = sb("yt", [P, 2, BPG, 16 * SEQ])
        qkt = yt[:].rearrange("p n a b -> p n (a b)").rearrange("p n (k t) -> p n k t", t=TOK)
        vt = sb("vt", [P, BPG, 8 * D])
        hidden = vt[:].rearrange("p b c -> p (b c)").rearrange("p (n c t) -> p n c t", n=2, t=TOK)
        xrow = sb("xrow", [P, 2, TPG, D])
        crow = sb("crow", [P, 2, TPG, CD])
        xt = [sb(f"xt_{n}", [P, 2, TOK], F32R) for n in ("hi", "lo")]
        ct = [sb(f"ct_{n}", [P, 2, TOK], F32R) for n in ("hi", "lo")]
        prob = sb("prob", [P, BPG, 512])
        pt = sb("pt", [P, BPG, 512])
        smax = sb("smax", [P, BPG, 8])
        ssum = sb("ssum", [P, BPG, 8])
        stats = sb("stats", [P, TPG, 6])
        moments = sb("moments", [P, TPG, 2])
        rstd = sb("rstd", [P, TPG])
        varp = sb("varp", [P, TPG])
        eps = sb("eps", [P, TPG])
        carrier = sb("carrier", [P, 1])
        mhalf = sb("mhalf", [P, TPG])
        orow = vt[:, 0:2, 4 * D:4 * D + TOK].rearrange("p n (t d) -> p n t d", d=D)
        kt = vt[:, 0:2, 4 * D + TOK:4 * D + 2 * TOK]
        mask_i = vt[:, 2:4, 4 * D:4 * D + TOK].bitcast(I32)
        qk_t = {a.name: [sb(f"qk_t_{a.name}_{n}", [P, 16, P], F32R) for n in ("hi", "lo")] for a in (SELF, CROSS)}
        fold_qk = [sb(f"fold_qk_{n}", [P, LAST.heads, CD], F32R) for n in ("hi", "lo")]
        fold_vo = {a.name: [sb(f"fold_vo_{a.name}_{n}", [P, a.heads, D], F32R) for n in ("hi", "lo")]
                   for a in (SELF, CROSS, LAST)}
        wg_t = [sb(f"wg_t_{n}", [P, 8, P], F32R) for n in ("hi", "lo")]
        wf_t = sb("wf_t", [P, 4, P])
        gains = [[sb(f"gain{i}", [P, D]), sb(f"bias{i}", [P, D])] for i in range(2)]
        out_bias = [sb(f"out_bias{i}", [P, D]) for i in range(3)]
        cols = sb("cols", [P, 8])
        row_eps = sb("row_eps", [P, TILES])
        raw_a = yt[:].rearrange("p a b c -> p (a b c)")
        raw_b = vt[:].rearrange("p b c -> p (b c)")
        raw_c = pt[:].rearrange("p b c -> p (b c)")

        jobs = []
        raws = []
        regions = {"a": raw_a, "b": raw_b, "c": raw_c}
        place = {"a": 0, "b": 0, "c": 0}

        def space(region, rows, shape, at=None):
            n = int(np.prod(shape))
            if at is None:
                at = place[region]
                place[region] += n
            assert at + n <= regions[region].shape[1]
            return regions[region][0:rows, at:at + n].rearrange("p (a b) -> p a b", a=shape[0])

        def raw(region, ap, rows, shape):
            view = space(region, rows, shape)
            raws.append((view, ap))
            return view, len(raws)

        def bank(n):
            return (ps_ring + ps_s)[n % 4]

        def turn4(src, rows, width, dst, loaded, scale=1.0):
            n = len(jobs)
            ps = bank(n)[0:width, 0:4 * rows].rearrange("p (k r) -> p k r", k=4)
            jobs.append((loaded, 0, [(ps[:, k, :], "turn", src(k), rows) for k in range(4)], [(dst, ps, scale)]))
            return n + 1

        def prep_l0(wq, wk, wv, wo, a, region, wot_at=None):
            wqr, l1 = raw(region, wq.rearrange("(t p) d -> p t d", p=P), P, [8, D])
            wkr, l2 = raw(region, wk.rearrange("(t p) d -> p t d", p=P), P, [8, a.kw])
            wvr, l3 = raw(region, wv.rearrange("(t p) d -> p t d", p=P), P, [8, a.kw])
            wor, l4 = raw(region, wo, P, [8, P])
            wot = space("a", P, [8, P], wot_at)
            dep = 0
            for c in range(2):
                dep = turn4(lambda k, c=c: wor[:, 4 * c + k, :], P, P, wot[:, 4 * c:4 * c + 4, :], l4)
            for c in range(2):
                for n, (src, width, scale) in enumerate(((wqr, P, 64 ** -0.5), (wkr, a.kw, 1.0))):
                    turn4(lambda k, c=c, src=src: src[:, 4 * c + k, :], P, width,
                          [w[0:width, 8 * c + n:8 * c + 8:2, :] for w in qk_t[a.name]], l4, scale)
            for c in range(4):
                o, r = c // 2, c % 2
                rows = slice(64 * o, 64 * o + 64)
                ps = bank(len(jobs))[0:a.kw, :].rearrange("p (k r) -> p k r", k=4)
                mm = [(ps[:, k, :], "mm", wvr[rows, m, :], wot[rows, m, :])
                      for k, m in enumerate((2 * r, 2 * r + 1, 4 + 2 * r, 5 + 2 * r))]
                at = 8 * r + 4 * o
                jobs.append((l4, dep, mm, [([w[0:a.kw, at:at + 4, :] for w in fold_vo[a.name]], ps, 1.0)]))

        def prep_last():
            wqr, l1 = raw("a", t["L1_xattn_Wq"], P, [8, P])
            wkr, l2 = raw("a", t["L1_xattn_Wk"], CD, [8, P])
            wvr, l3 = raw("a", t["L1_xattn_Wv"], CD, [8, P])
            wor, l4 = raw("c", t["L1_xattn_Wo"].rearrange("(t p) d -> p t d", p=P), P, [8, P])
            wgr, l5 = raw("c", t["L0_xattn_w_geglu"].rearrange("(t p) d -> p t d", p=P), P, [8, P])
            wfr, l6 = raw("b", t["L0_xattn_w_ffout"], P, [4, P])
            wqt, wkt, wvt = (space("a", P, [8, n], (k + 1) * 8 * P) for k, n in enumerate((P, CD, CD)))
            for c in range(2):
                for src, rows, dst in ((wqr, P, wqt), (wkr, CD, wkt), (wvr, CD, wvt)):
                    dep = turn4(lambda k, c=c, src=src: src[:, 4 * c + k, :], rows, P, dst[:, 4 * c:4 * c + 4, :], l6)
            for c in range(2):
                ps = bank(len(jobs))[:, 0:4 * CD].rearrange("p (k r) -> p k r", k=4)
                jobs.append((l6, dep, [(ps[:, k, :], "mm", wqt[:, 4 * c + k, :], wkt[:, 4 * c + k, :]) for k in range(4)],
                             [([w[:, 4 * c:4 * c + 4, :] for w in fold_qk], ps, 128 ** -0.5)]))
            for c in range(2):
                ps = bank(len(jobs))[0:CD, :].rearrange("p (k r) -> p k r", k=4)
                jobs.append((l6, dep, [(ps[:, k, :], "mm", wvt[:, h, :], wor[:, h, :])
                                       for k, h in enumerate((2 * c, 2 * c + 1, 4 + 2 * c, 5 + 2 * c))],
                             [([w[0:CD, 4 * c:4 * c + 4, :] for w in fold_vo["last"]], ps, 1.0)]))
            for c in range(2):
                turn4(lambda k, c=c: wgr[:, 4 * c + k, :], P, P, [w[:, 4 * c:4 * c + 4, :] for w in wg_t], l6)
            turn4(lambda k: wfr[:, k, :], P, P, wf_t[:, :, :], l6)

        prep_l0(t["L0_xattn_wq1"], t["L0_xattn_wk1"], t["L0_xattn_wv1"], t["L0_xattn_wo1"], SELF, "a")
        first_raws = len(raws)
        prep_l0(t["L0_xattn_wq2"], t["L0_xattn_wk2"], t["L0_xattn_wv2"], t["L0_xattn_wo2"], CROSS, "b", 0)
        second_raws = len(raws)
        prep_last()

        s_raw = [sem(f"s_raw{i}") for i in range(3)]
        s_small = sem("s_small")
        s_gains = [sem("s_gains_ffn"), sem("s_gains_last")]
        s_x = [sem("s_x_first"), sem("s_x_rest")]
        prep_ready = sem("prep_ready")
        prep_copied = sem("prep_copied")
        prep_high = sem("prep_high")
        set_end = [first_raws, second_raws, len(raws)]
        set_sem = [0 if n < first_raws else 1 if n < second_raws else 2 for n in range(len(raws))]

        def raw_loaded(eng, n):
            k = set_sem[n - 1]
            eng.wait_ge(s_raw[k], 16 * (set_end[k] - (set_end[k - 1] if k else 0)))

        mask_h = prob[:, 0, 0:SEQ].bitcast(I32)
        has_key = prob[:, 0, SEQ:2 * SEQ]
        ones = prob[:, 0, 2 * SEQ:3 * SEQ]
        any_key = prob[:, 0, 3 * SEQ:3 * SEQ + 1]
        key_sel = prob[:, 1, 0:2 * TILES].rearrange("p (b t) -> p b t", b=2)
        last_eps = prob[:, 1, 2 * TILES:3 * TILES]
        keys_spread = sem("keys_spread")
        s_ones_row = sem("s_ones_row")
        s_mask = sem("s_mask")
        s_bad = sem("s_bad")
        s_const = sem("s_const")

        phases = {}

        def phase_sems(name, names):
            phases[name] = {n: sem(f"{name}_{n}") for n in names}
            return phases[name]

        common = ["ring_done", "ring_high", "ring_free0", "ring_free1", "resid_done", "rows_ready"]
        norm = ["stat", "var_ready", "scaled_ready", "rstd_ready", "norm_ready", "gain_done"]
        attn = ["scores_done", "max_done", "shifted", "exp_done", "sum_done", "recip_done", "prob_ready", "turned",
                "pt_copied", "v_done", "v_copied0", "pv_done"]
        ctx = ["crow0", "crow1"]
        sems = {"self": phase_sems("self", common + norm + attn + ["v_copied1", "biased"]),
                "cross": phase_sems("cross", common + norm + attn + ctx + ["v_copied1", "biased"]),
                "ffn": phase_sems("ffn", common + norm + ["up_done", "gate_done", "h_done", "o_done", "biased"]),
                "last": phase_sems("last", common + attn + ctx + [
                    "mask0", "mask1", "mask_done", "out0", "out1", "scaled_ready", "fin_stat", "fin_var", "fin_rstd",
                    "fin_norm", "fin_gain", "fin_done"])}
        before = {"self": None, "cross": "self", "ffn": "cross", "last": "ffn"}

        def phase_begins(eng, name):
            if before[name]:
                eng.wait_ge(sems[before[name]]["resid_done"], NG)

        def ring_at(g, ring, k):
            n0 = ring * g.base + k
            uses = n0 // 2 if g.i is None else g.i * ring + n0 // 2
            return n0 % 2, uses

        s_ident = sem("s_ident")

        block = stack.enter_context(nc.Block())

        @block.sync
        def _(sp):
            def load_set(k):
                lo = set_end[k - 1] if k else 0
                for view, ap in raws[lo:set_end[k]]:
                    dst = view
                    if len(ap.shape) == 2 and len(view.shape) == 3:
                        dst = view.rearrange("p a b -> p (a b)")
                    sp.dma_start(dst, ap).then_inc(s_raw[k], 16)

            xr = t["x"].rearrange("b s d -> (b s) d").rearrange("(t p) d -> p t d", p=P)
            cr = t["ctx_768"].rearrange("b s d -> (b s) d").rearrange("(t p) d -> p t d", p=P)
            orows = out.rearrange("b s d -> (b s) d").rearrange("(t p) d -> p t d", p=P)
            mr = t["mask_BxS2_if1"].rearrange("(a b) s -> a (b s)", a=1)
            first = 4 * TPG
            load_set(0)
            sp.dma_start(x[:, 0:first, :], xr[:, 0:first, :]).then_inc(s_x[0], 16)
            def load_gains(i, names, loaded):
                for dst, n in zip(gains[i], names):
                    sp.dma_start(dst[:], t[n].rearrange("(a d) -> a d", a=1).to_broadcast([P, D])).then_inc(loaded, 16)

            load_gains(0, ("L0_xattn_ln1_g", "L0_xattn_ln1_b"), s_small)
            load_gains(1, ("L0_xattn_ln2_g", "L0_xattn_ln2_b"), s_small)
            for dst, n in zip(out_bias, ("L0_xattn_bo1", "L0_xattn_bo2", "L0_xattn_b_ffout")):
                sp.dma_start(dst[:], t[n].rearrange("(a d) -> a d", a=1).to_broadcast([P, D])).then_inc(s_small, 16)
            for c in range(8):
                sp.dma_start(cols[:, c:c + 1], t["L0_xattn_b_geglu"][c * P:(c + 1) * P].rearrange("(d a) -> d a", a=1)).then_inc(s_small, 16)
            load_set(1)
            load_set(2)
            sp.dma_start(x[:, first:TILES, :], xr[:, first:TILES, :]).then_inc(s_x[1], 16)
            sp.dma_start(mask_h, t["mask_BxS2_if1"]).then_inc(s_mask, 16)

            for a in (CROSS, LAST):
                s = sems[a.name]
                if a is LAST:
                    phase_begins(sp, "ffn")
                    load_gains(1, ("L1_xattn_gamma", "L1_xattn_beta"), s_gains[1])
                phase_begins(sp, a.name)
                if a is CROSS:
                    load_gains(0, ("L0_xattn_ln3_g", "L0_xattn_ln3_b"), s_gains[0])

                def body(g):
                    nxt, og = g.plus(2), g.plus(-2)

                    def known(v):
                        return v if isinstance(v, int) else sp.snap(v)

                    tile, turned = known(nxt.at(TPG)), known(g.at(a.ring, 1))
                    if a.mask:
                        token, masked = known(nxt.at(TOK)), known(g.at(1, 1))
                        otile, finished = known(og.at(TPG)), known(og.at(1, 1))

                    if nxt:
                        if g:
                            sp.wait_ge(s["ring_done"], turned)
                        sp.dma_start(crow[:, g.par, :, :], cr[:, bass.ds(tile, TPG), :]).then_inc(s[f"crow{g.par}"], 16)
                    if nxt and a.mask:
                        if g:
                            sp.wait_ge(s["mask_done"], masked)
                        sp.dma_start(mask_i[96:97, g.par, :], mr[:, bass.ds(token, TOK)]).then_inc(s[f"mask{g.par}"], 16)
                    if og and a.mask:
                        sp.wait_ge(s["fin_done"], finished)
                        sp.dma_start(orows[:, bass.ds(otile, TPG), :], orow[:, og.par, :, :]).then_inc(s[f"out{og.par}"], 16)
                over_groups(sp, body)
            for p in range(2):
                sp.wait_ge(sems["last"][f"out{p}"], 16 * (NG // 2))

        @block.tensor
        def _(pe):
            pe.wait_ge(s_ident, 2)
            for n, (loaded, dep, mm, _) in enumerate(jobs):
                raw_loaded(pe, loaded)
                wait(pe, prep_copied, max(n - 3, dep))
                for o, kind, a, b in mm:
                    if kind == "turn":
                        last = pe.transpose(o, a, ident[0:b, 0:b])
                    else:
                        last = pe.matmul(o, a, b, start=True, stop=True)
                last.then_inc(prep_ready, 1)
            pe.wait_ge(s_bad, 5)
            for b2 in range(2):
                last = pe.matmul(ps_pt[64 * b2:64 * b2 + 64, 0:TILES], ones, key_sel[:, b2, :], start=True, stop=True)
            last.then_inc(keys_spread, 1)
            pe.wait_ge(s_bad, 6)
            pe.wait_ge(prep_copied, len(jobs))

            def head_bank(s, g, ring, a):
                bank_, uses = ring_at(g, ring, 0)
                wait(pe, s[f"ring_free{bank_}"], uses)
                pe.wait_ge(s["rows_ready"], g.at(1, 1))
                for k in range(TPG):
                    last = pe.transpose(ps_ring[bank_][:, k * P:(k + 1) * P], xrow[:, g.par, k, :], ident[:, :])
                if a is not None and a.ctx:
                    pe.wait_ge(s[f"crow{g.par}"], g.half(16, 16))
                    for k in range(TPG):
                        last = pe.transpose(ps_ring[bank_][0:CD, TOK + k * P:TOK + (k + 1) * P], crow[:, g.par, k, :], ident[:, :])
                last.then_inc(s["ring_done"], 1)

            def attention(a):
                s = sems[a.name]
                wqk, wvo = qk_t[a.name] if a.narrow else fold_qk, fold_vo[a.name]

                def scores_waits(g, b):
                    if b == 0:
                        for k in (a.pairs - 1, a.pairs):
                            bank_, uses = ring_at(g, a.ring, k)
                            pe.wait_ge(s[f"ring_free{bank_}"], uses + 1)
                        if a.mask:
                            pe.wait_ge(s["mask_done"], g.at(1, 1))
                            if g.i is None and g.base == 0:
                                pe.wait_ge(s_ones_row, 3)
                    wait(pe, s["shifted"], g.at(BPG, b if a.narrow else b - 1))

                def scores(g, b):
                    if a.narrow:
                        tokens = slice(b * SEQ, (b + 1) * SEQ)
                        for q in range(a.pairs):
                            for r in range(2):
                                rows = slice(64 * r, 64 * r + 64)
                                last = pe.matmul(ps_s[r][64 * (q % 2):64 * (q % 2) + 64, q // 2 * SEQ:(q // 2 + 1) * SEQ],
                                                 qkt[rows, g.par, 2 * q, tokens], qkt[rows, g.par, 2 * q + 1, tokens],
                                                 start=True, stop=True)
                        last.then_inc(s["scores_done"], 1)
                        return
                    for h in range(a.heads):
                        last = pe.matmul(ps_s[b % 2][64 * (h % 2):64 * (h % 2) + 64, h // 2 * SEQ:(h // 2 + 1) * SEQ],
                                         yt[0:a.kw + 1, g.par, b, h * SEQ:(h + 1) * SEQ],
                                         kt[0:a.kw + 1, g.par, b * SEQ:(b + 1) * SEQ], start=True, stop=True)
                    last.then_inc(s["scores_done"], 1)

                def queries(g, k):
                    bank_, uses = ring_at(g, a.ring, k + 1)
                    wait(pe, s[f"ring_free{bank_}"], uses)
                    if k == 0:
                        hb, huses = ring_at(g, a.ring, 0)
                        pe.wait_ge(s[f"ring_free{hb}"], huses + 1)
                    for j in range(2):
                        of, rows = (ct, a.kw) if a.narrow and a.ctx and j == 1 else (xt, P)
                        last = matmul3(pe, ps_ring[bank_][0:a.qrows, j * TOK:(j + 1) * TOK],
                                       [w[0:rows, 2 * k + j, :] for w in wqk], [v[0:rows, g.par, :] for v in of])
                    last.then_inc(s["ring_done"], 1)

                def turn_probs(g, b):
                    pe.wait_ge(s["prob_ready"], g.at(BPG, b + 1))
                    wait(pe, s["pt_copied"], g.at(BPG, b))
                    for k in range(a.turns):
                        last = pe.transpose(ps_pt[:, k * P:(k + 1) * P], prob[:, b, k * P:(k + 1) * P], ident[:, :])
                    last.then_inc(s["turned"], 1)

                def values(g, b):
                    keys = ct if a.ctx else xt
                    tokens = slice(b // 2 * P, b // 2 * P + P)
                    for r in (0, 1) if a.narrow else (b % 2,):
                        if a.narrow:
                            wait(pe, s[f"v_copied{r}"], g.at(BPG, b))
                        else:
                            wait(pe, s["v_copied0"], g.at(BPG, b - 1))
                        at = r * a.heads // 2 + (4 * (b % 2) if a.narrow else 0)
                        last = matmul3(pe, ps_v[r][:, :], [v[0:a.kw, g.par, tokens] for v in keys],
                                       [w[0:a.kw, at:at + 4, :].rearrange("e k d -> e (k d)") for w in wvo])
                        last.then_inc(s["v_done"], 1)

                def output(g, pair):
                    odd = 2 * pair + 1
                    if pair == 0:
                        wait(pe, s["resid_done"], g.at(1))
                    pe.wait_ge(s["pt_copied"], g.at(BPG, odd + 1))
                    for c in range(2 if a.narrow else 1):
                        pe.wait_ge(s[f"v_copied{c}"], g.at(BPG, odd + 1))
                    for j in range(a.pairs):
                        for e in range(2):
                            last = pe.matmul(ps_o[64 * e:64 * e + 64, pair * D:(pair + 1) * D],
                                             pt[:, 2 * pair + e, j * SEQ:(j + 1) * SEQ],
                                             vt[:, 2 * pair + e, j * D:(j + 1) * D],
                                             start=(j == 0), stop=(j == a.pairs - 1))
                    last.then_inc(s["pv_done"], 1)

                def body(g):
                    for b in range(BPG):
                        if g:
                            if not a.narrow:
                                scores_waits(g, b)
                            scores(g, b)
                        fill = list(a.fills[b]) if g.plus(1) else []
                        for k in fill[0:2]:
                            queries(g.plus(1), k)
                        tg, tb = back(g, b, 2)
                        if tg:
                            turn_probs(tg, tb)
                        for k in fill[2:]:
                            queries(g.plus(1), k)
                        if b % 2 == 0 and g.plus(-1):
                            output(g.plus(-1), b // 2)
                        if a.narrow and b < BPG - 1 and g:
                            scores_waits(g, b + 1)
                        if g:
                            values(g, b)
                        if a.narrow and b == BPG - 1 and g.plus(1):
                            scores_waits(g.plus(1), 0)
                        if b == BPG - 1 and g.plus(2):
                            head_bank(s, g.plus(2), a.ring, a)
                over_groups(pe, body)

            def ffn():
                s = sems["ffn"]

                def up(g):
                    hb, huses = ring_at(g, 1, 0)
                    pe.wait_ge(s[f"ring_free{hb}"], huses + 1)
                    for c in range(4):
                        dst = (ps_s[0], ps_s[1], ps_v[0], ps_v[1])[c]
                        wait(pe, s["h_done"], g.at(4, c - 3))
                        v = [v[:, g.par, :] for v in xt]
                        matmul3(pe, dst[:, 0:TOK], [w[:, 4 + c, :] for w in wg_t], v)
                        matmul3(pe, dst[:, TOK:2 * TOK], [w[:, c, :] for w in wg_t], v).then_inc(s["up_done"], 1)

                def down(g):
                    pe.wait_ge(s["h_done"], g.at(4, 4))
                    wait(pe, s["resid_done"], g.at(1, -1))
                    for k in range(TPG):
                        for c in range(4):
                            last = pe.matmul(ps_down[g.par][:, k * D:(k + 1) * D], hidden[:, g.par, c, k * P:(k + 1) * P],
                                             wf_t[:, c, :], start=(c == 0), stop=(c == 3))
                    last.then_inc(s["o_done"], 1)

                def body(g):
                    if g.plus(-1):
                        down(g.plus(-1))
                    if g.plus(1):
                        up(g.plus(1))
                    if g.plus(2):
                        head_bank(s, g.plus(2), 1, None)
                over_groups(pe, body, lead=3)

            for name, run in (("self", lambda: attention(SELF)), ("cross", lambda: attention(CROSS)),
                              ("ffn", ffn), ("last", lambda: attention(LAST))):
                phase_begins(pe, name)
                run()

        def ring_out(eng, copy, s, g, a, k):
            bank_, uses = ring_at(g, a.ring, k)
            eng.wait_ge(s["ring_done"], g.at(a.ring, k + 1))
            if a.narrow:
                copy(qkt[:, g.par, 2 * k - 2:2 * k, :].rearrange("p k t -> p (k t)"), ps_ring[bank_][:, :])\
                    .then_inc(s[f"ring_free{bank_}"], 1)
                return
            copy(yt[0:a.kw, g.par, :, (2 * k - 2) * SEQ:2 * k * SEQ].rearrange("p b (h i) -> p b h i", h=2),
                 ps_ring[bank_][0:a.kw, :].rearrange("p (h b i) -> p b h i", h=2, b=BPG)).then_inc(s[f"ring_free{bank_}"], 1)

        def ring_step(eng, copy, s, g, b, a, which):
            for k in which:
                if g.plus(1) and k < len(a.fills[b]):
                    ring_out(eng, copy, s, g.plus(1), a, a.fills[b][k] + 1)

        def values_out(eng, copy, s, g, b, a, r):
            vg, vb = back(g, b, 1)
            if vg:
                banks = a.heads // 8
                eng.wait_ge(s["v_done"], vg.at(BPG * banks, vb * banks + r + 1))
                at = 4 * D * (vb % 2) if a.narrow else 0
                bank_ = r
                if not a.narrow:
                    r = vb % 2
                for e in range(2):
                    ins = copy(vt[64 * r:64 * r + 64, vb // 2 * 2 + e, at:at + 4 * D], ps_v[r][64 * e:64 * e + 64, :])
                ins.then_inc(s[f"v_copied{bank_}"], 1)

        def head_ring(a):
            return a.ring if a else 1

        @block.scalar
        def _(act):
            def copy(dst, src):
                return act.activation(dst, src, ACT.Copy)

            def head_high(s, g, a):
                if not g:
                    return
                bank_, uses = ring_at(g, head_ring(a), 0)
                act.wait_ge(s["ring_done"], g.at(head_ring(a), 1))
                ps = ps_ring[bank_]
                ins = copy(xt[0][:, g.par, :], ps[:, 0:TOK])
                if a and a.ctx:
                    ins = copy(ct[0][0:a.kw, g.par, :], ps[0:a.kw, TOK:2 * TOK])
                    if a.mask:
                        ins = copy(kt[0:a.kw, g.par, :], ps[0:a.kw, TOK:2 * TOK])
                ins.then_inc(s["ring_high"], 1)

            for n, (_, _, _, outs) in enumerate(jobs):
                (dst, src, scale), = outs
                if isinstance(dst, list):
                    act.wait_ge(prep_ready, n + 1)
                    act.activation(dst[0], src, ACT.Copy, scale=scale).then_inc(prep_high, 1)
                elif n % 2:
                    act.wait_ge(prep_ready, n + 1)
                    act.wait_ge(prep_copied, n)
                    act.activation(dst, src, ACT.Copy, scale=scale).then_inc(prep_copied, 1)
            act.wait_ge(s_small, 16 * SMALL)

            def attention(a):
                s = sems[a.name]

                def body(g):
                    for b in range(BPG):
                        values_out(act, copy, s, g, b, a, 0)
                        if b == 0:
                            head_high(s, g.plus(1), a)
                        ring_step(act, copy, s, g, b, a, [0])
                        if g:
                            act.wait_ge(s["shifted"], g.at(BPG, b + 1))
                            act.activation(prob[:, b, 0:a.pairs * SEQ], prob[:, b, 0:a.pairs * SEQ], ACT.Exp)\
                               .then_inc(s["exp_done"], 1)
                        tg, tb = back(g, b, 2)
                        if tg:
                            act.wait_ge(s["turned"], tg.at(BPG, tb + 1))
                            copy(pt[:, tb, 0:a.turns * P], ps_pt[:, 0:a.turns * P]).then_inc(s["pt_copied"], 1)
                        ring_step(act, copy, s, g, b, a, [2, 3] if a.narrow else [1])
                over_groups(act, body)

            def ffn():
                s = sems["ffn"]

                def body(g):
                    if g.plus(1):
                        n = g.plus(1)
                        for c in range(4):
                            act.wait_ge(s["up_done"], n.at(4, c + 1))
                            wait(act, s["h_done"], n.at(4, c - 3))
                            act.activation(yt[:, 0, c, 0:TOK], (ps_s[0], ps_s[1], ps_v[0], ps_v[1])[c][:, 0:TOK],
                                           ACT.Gelu, bias=cols[:, 4 + c:5 + c]).then_inc(s["gate_done"], 1)
                    head_high(s, g.plus(2), None)
                over_groups(act, body, lead=3)

            for name, run in (("self", lambda: attention(SELF)), ("cross", lambda: attention(CROSS)),
                              ("ffn", ffn), ("last", lambda: attention(LAST))):
                phase_begins(act, name)
                run()

        @block.vector
        def _(dve):
            def copy(dst, src):
                return dve.tensor_copy(dst, src)

            def low(dst, whole, high):
                return dve.tensor_tensor(dst, whole, high, ALU.subtract)

            def head_low(s, g, a):
                if not g:
                    return
                bank_, uses = ring_at(g, head_ring(a), 0)
                dve.wait_ge(s["ring_high"], g.at(1, 1))
                ins = low(xt[1][:, g.par, :], ps_ring[bank_][:, 0:TOK], xt[0][:, g.par, :])
                if a and a.ctx:
                    ins = low(ct[1][0:a.kw, g.par, :], ps_ring[bank_][0:a.kw, TOK:2 * TOK], ct[0][0:a.kw, g.par, :])
                ins.then_inc(s[f"ring_free{bank_}"], 1)

            dve.memset(mhalf[:], -0.5).then_inc(s_const, 1)
            dve.memset(eps[:], EPS).then_inc(s_const, 1)
            split = 0
            for n, (_, _, _, outs) in enumerate(jobs):
                (dst, src, scale), = outs
                if isinstance(dst, list):
                    split += 1
                    dve.wait_ge(prep_high, split)
                    dve.scalar_tensor_tensor(out=dst[1], in0=src, scalar=scale, in1=dst[0], op0=ALU.mult,
                                             op1=ALU.subtract).then_inc(prep_copied, 1)
                elif n % 2 == 0:
                    dve.wait_ge(prep_ready, n + 1)
                    wait(dve, prep_copied, n)
                    dve.tensor_scalar(dst, src, scale, None, ALU.mult).then_inc(prep_copied, 1)
            dve.wait_ge(s_mask, 16)
            dve.tensor_scalar(has_key, mask_h, 0.0, None, ALU.not_equal).then_inc(s_bad, 1)
            dve.wait_ge(s_bad, 1)
            dve.tensor_reduce(any_key, has_key, AX_X, ALU.max).then_inc(s_bad, 1)
            dve.memset(ones, 1.0).then_inc(s_bad, 1)
            dve.wait_ge(s_bad, 3)
            dve.wait_ge(s_ident, 2)
            for b2 in range(2):
                dve.tensor_scalar(key_sel[:, b2, :], ident[:, b2:P:2], any_key[:, 0:1], None, ALU.mult).then_inc(s_bad, 1)
            dve.wait_ge(keys_spread, 1)
            dve.tensor_scalar(last_eps, ps_pt[:, 0:TILES], 0.0, -3e38, ALU.is_equal, ALU.mult).then_inc(s_bad, 1)
            dve.wait_ge(s_bad, 6)
            dve.tensor_scalar(row_eps[:], last_eps, 10.0, None, ALU.mult).then_inc(s_bad, 1)
            dve.wait_ge(s_bad, 7)
            dve.tensor_tensor(last_eps, row_eps[:], row_eps[:], ALU.subtract).then_inc(s_bad, 1)
            dve.wait_ge(s_bad, 8)
            dve.tensor_scalar(row_eps[:], last_eps, EPS, None, ALU.add).then_inc(s_bad, 1)
            dve.wait_ge(s_x[0], 16)
            dve.wait_ge(s_small, 16 * SMALL)

            def norm_stats(s, g, src, stat, var):
                for k in range(TPG):
                    dve.bn_stats(stats[:, k, :], src(k)).then_inc(s[stat], 1)
                dve.wait_ge(s[stat], g.at(TPG + 1, TPG))
                dve.memset(carrier[:], 0.0).then_inc(s[stat], 1)
                for k in range(TPG):
                    ins = dve.bn_aggr(moments[:, k, :], stats[:, k, :])
                ins.then_inc(s[var], 1)

            def norm_rows(s, g, src, dst, rst, done):
                dve.wait_ge(s[rst], g.at(1, 1))
                for k in range(TPG):
                    ins = dve.tensor_scalar(dst(k), src(k), moments[:, k, 0:1], rstd[:, k:k + 1], ALU.subtract, ALU.mult)
                ins.then_inc(s[done], 1)

            def ln_stats(s, g):
                norm_stats(s, g, lambda k: x[:, bass.ds(g.at(TPG, k), 1), :].rearrange("p a d -> p (a d)"), "stat", "var_ready")

            def ln_rows(s, g, ring):
                if g.i is not None or g.base >= 2:
                    dve.wait_ge(s["ring_done"], g.at(ring, 1 - 2 * ring))
                norm_rows(s, g, lambda k: x[:, bass.ds(g.at(TPG, k), 1), :].rearrange("p a d -> p (a d)"),
                          lambda k: xrow[:, g.par, k, :], "rstd_ready", "norm_ready")

            def residual(s, g, rows):
                xs = x[:, bass.ds(g.at(TPG), TPG), :].rearrange("p t d -> p (t d)")
                dve.tensor_tensor(xs, rows, xs, ALU.add).then_inc(s["resid_done"], 1)

            def final_rows(s, g):
                dve.wait_ge(s["pv_done"], g.at(2, 2))
                if g.i is not None or g.base >= 2:
                    dve.wait_ge(s[f"out{g.par}"], g.half(16))
                o = orow[:, g.par, :, :].rearrange("p t d -> p (t d)")
                xs = x[:, bass.ds(g.at(TPG), TPG), :].rearrange("p t d -> p (t d)")
                dve.tensor_tensor(o, ps_o[:, 0:TOK], xs, ALU.add).then_inc(s["resid_done"], 1)

            def final_stats(s, g):
                dve.wait_ge(s["resid_done"], g.at(1, 1))
                norm_stats(s, g, lambda k: orow[:, g.par, k, :], "fin_stat", "fin_var")

            def final_norm(s, g):
                norm_rows(s, g, lambda k: orow[:, g.par, k, :], lambda k: orow[:, g.par, k, :], "fin_rstd", "fin_norm")

            def attention(a):
                s = sems[a.name]
                n = a.pairs * SEQ

                def body(g):
                    for b in range(BPG):
                        if a.narrow:
                            values_out(dve, copy, s, g, b, a, 1)
                        if g:
                            banks = 2 if a.narrow else 1
                            pb = prob[:, b, 0:n].rearrange("p (o q j) -> p o q j", o=banks, j=SEQ)
                            ps = (ps_scores[:, :, 0:n // 2] if a.narrow else ps_scores[:, b % 2:b % 2 + 1, 0:n])\
                                .rearrange("p o (q j) -> p o q j", j=SEQ)
                            top = smax[:, b, 0:a.pairs].rearrange("p (o q) -> p o q", o=banks)
                            dve.wait_ge(s["scores_done"], g.at(BPG, b + 1))
                            dve.tensor_reduce(top, ps, AX_X, ALU.max).then_inc(s["max_done"], 1)
                            dve.wait_ge(s["max_done"], g.at(BPG, b + 1))
                            wait(dve, s["turned"], g.at(BPG, b - 3))
                            dve.tensor_tensor(pb, ps, top.unsqueeze(3).to_broadcast([P, banks, a.pairs // banks, SEQ]),
                                              ALU.subtract).then_inc(s["shifted"], 1)
                        if b == 0:
                            head_low(s, g.plus(1), a)
                        if a.narrow:
                            ring_step(dve, copy, s, g, b, a, [1])
                        if b == 3 and g.plus(-1):
                            if a.mask:
                                final_rows(s, g.plus(-1))
                            else:
                                dve.wait_ge(s["pv_done"], g.plus(-1).at(2, 2))
                                dve.wait_ge(s["biased"], g.at(1))
                                residual(s, g.plus(-1), ps_o[:, 0:TOK])
                        if b == 0 and g.plus(-2) and a.mask:
                            final_stats(s, g.plus(-2))
                        if b == 1 and g.plus(-2) and a.mask:
                            final_norm(s, g.plus(-2))
                        if g:
                            dve.wait_ge(s["exp_done"], g.at(BPG, b + 1))
                            pb = prob[:, b, 0:n].rearrange("p (q j) -> p q j", j=SEQ)
                            dve.tensor_reduce(ssum[:, b, 0:a.pairs], pb, AX_X, ALU.add).then_inc(s["sum_done"], 1)
                            dve.wait_ge(s["sum_done"], g.at(BPG, b + 1))
                            dve.reciprocal(ssum[:, b, 0:a.pairs], ssum[:, b, 0:a.pairs]).then_inc(s["recip_done"], 1)
                        if b == 0 and g.plus(2) and a.ln:
                            ln_stats(s, g.plus(2))
                        if b == 1 and g.plus(2) and a.ln:
                            ln_rows(s, g.plus(2), a.ring)
                    nxt = g.plus(2)
                    if nxt and a.mask:
                        dve.wait_ge(s[f"mask{nxt.par}"], nxt.half(16, 16))
                        if g:
                            dve.wait_ge(s["scores_done"], g.at(BPG, BPG))
                        dve.tensor_scalar(kt[96:97, g.par, :], mask_i[96:97, g.par, :], 0.0, MASKED,
                                          ALU.is_equal, ALU.mult).then_inc(s["mask_done"], 1)
                over_groups(dve, body, before_loop=(lambda: dve.wait_ge(s_x[1], 16)) if a is SELF else None)

            def ffn():
                s = sems["ffn"]

                def body(g):
                    if g.plus(-2):
                        dve.wait_ge(s["o_done"], g.at(1, -1))
                        dve.wait_ge(s["biased"], g.at(1, -1))
                        residual(s, g.plus(-2), ps_down[g.par][:, 0:TOK])
                    if g.plus(3):
                        ln_stats(s, g.plus(3))
                    for c in range(4):
                        if c == 2 and g.plus(3):
                            ln_rows(s, g.plus(3), 1)
                        if g.plus(1):
                            n = g.plus(1)
                            dve.wait_ge(s["gate_done"], n.at(4, c + 1))
                            if c == 0:
                                wait(dve, s["o_done"], n.at(1, -1))
                            dve.scalar_tensor_tensor(out=hidden[:, n.par, c, :], in0=(ps_s[0], ps_s[1], ps_v[0], ps_v[1])[c][:, TOK:2 * TOK],
                                                     scalar=cols[:, c:c + 1], in1=yt[:, 0, c, 0:TOK],
                                                     op0=ALU.add, op1=ALU.mult).then_inc(s["h_done"], 1)
                    head_low(s, g.plus(2), None)
                over_groups(dve, body, lead=3)

            for name, run in (("self", lambda: attention(SELF)), ("cross", lambda: attention(CROSS)),
                              ("ffn", ffn), ("last", lambda: attention(LAST))):
                phase_begins(dve, name)
                run()

        @block.gpsimd
        def _(pool):
            pool.memset(ident[:], 0.0).then_inc(s_ident, 1)
            pool.wait_ge(s_ident, 1)
            pool.affine_select(out=ident[:], in_=ident[:], compare_op=ALU.not_equal, fill=1.0, base=0,
                               pattern=[[-1, P]], channel_multiplier=1).then_inc(s_ident, 1)
            pool.wait_ge(s_const, 2)
            pool.wait_ge(s_small, 16 * SMALL)
            pool.wait_ge(s_bad, 9)

            def root(s, g, var, scaled, rst, row_eps=None):
                pool.wait_ge(s[var], g.at(1, 1))
                e = eps[:] if row_eps is None else row_eps[:, bass.ds(g.at(TPG), TPG)]
                pool.tensor_tensor(varp[:], moments[:, :, 1], e, ALU.add).then_inc(s[scaled], 1)
                pool.wait_ge(s[scaled], g.at(1, 1))
                pool.tensor_tensor(rstd[:], varp[:], mhalf[:], ALU.pow).then_inc(s[rst], 1)

            def affine(s, g, rows, gain, bias, norm, gained, done):
                pool.wait_ge(s[norm], g.at(1, 1))
                pool.tensor_tensor(rows, rows, gain[:].unsqueeze(1).to_broadcast([P, TPG, D]), ALU.mult).then_inc(s[gained], 1)
                pool.wait_ge(s[gained], g.at(1, 1))
                pool.tensor_tensor(rows, rows, bias[:].unsqueeze(1).to_broadcast([P, TPG, D]), ALU.add).then_inc(s[done], 1)

            def add_bias(s, g, out_bias):
                xs = x[:, bass.ds(g.at(TPG), TPG), :]
                pool.tensor_tensor(xs, xs, out_bias[:].unsqueeze(1).to_broadcast([P, TPG, D]), ALU.add)\
                    .then_inc(s["biased"], 1)

            def attention(a, gain, bias, out_bias=None):
                s = sems[a.name]
                n = a.pairs * SEQ
                if a.mask:
                    pool.wait_ge(s_gains[1], 32)
                    pool.memset(yt[96:97, 0, :, 0:TOK], 1.0).then_inc(s_ones_row, 1)
                    pool.wait_ge(s_ones_row, 3)

                def body(g):
                    nxt = g.plus(2)
                    for b in range(BPG):
                        if a.mask and b == 0 and g.plus(-2):
                            root(s, g.plus(-2), "fin_var", "scaled_ready", "fin_rstd", row_eps)
                        if g:
                            pool.wait_ge(s["recip_done"], g.at(BPG, b + 1))
                            pb = prob[:, b, 0:n].rearrange("p (q j) -> p q j", j=SEQ)
                            pool.tensor_tensor(pb, pb, ssum[:, b, 0:a.pairs].unsqueeze(2).to_broadcast([P, a.pairs, SEQ]),
                                               ALU.mult).then_inc(s["prob_ready"], 1)
                        if a.mask and g.plus(-2):
                            og = g.plus(-2)
                            if b == 1:
                                affine(s, og, orow[:, og.par, :, :], gain, bias, "fin_norm", "fin_gain", "fin_done")
                        if nxt and a.ln and b == 0:
                            root(s, nxt, "var_ready", "scaled_ready", "rstd_ready")
                        if nxt and a.ln and b == 1:
                            affine(s, nxt, xrow[:, g.par, :, :], gain, bias, "norm_ready", "gain_done", "rows_ready")
                            add_bias(s, nxt, out_bias)
                        if nxt and not a.ln and b == 1:
                            if g:
                                pool.wait_ge(s["ring_done"], g.at(a.ring, 1))
                            pool.tensor_copy(xrow[:, g.par, :, :], x[:, bass.ds(nxt.at(TPG), TPG), :]).then_inc(s["rows_ready"], 1)
                over_groups(pool, body)

            def ffn():
                s = sems["ffn"]

                def body(g):
                    n = g.plus(3)
                    if n:
                        root(s, n, "var_ready", "scaled_ready", "rstd_ready")
                        affine(s, n, xrow[:, n.par, :, :], *gains[0], "norm_ready", "gain_done", "rows_ready")
                        add_bias(s, n, out_bias[2])
                pool.memset(yt[96:97, 1, :, 0:LAST.heads * SEQ], 1.0).then_inc(s_ones_row, 1)
                pool.wait_ge(s_ones_row, 1)
                pool.memset(yt[96:97, 0, :, TOK:LAST.heads * SEQ], 1.0).then_inc(s_ones_row, 1)
                pool.wait_ge(s_ones_row, 2)
                pool.wait_ge(s_gains[0], 32)
                over_groups(pool, body, lead=3)

            for name, run in (("self", lambda: attention(SELF, *gains[0], out_bias[0])),
                              ("cross", lambda: attention(CROSS, *gains[1], out_bias[1])),
                              ("ffn", ffn), ("last", lambda: attention(LAST, *gains[1]))):
                phase_begins(pool, name)
                run()


INPUTS = ["x", "ctx_768", "mask_BxS2_if1", "L0_xattn_wq1", "L0_xattn_wk1", "L0_xattn_wv1", "L0_xattn_wo1", "L0_xattn_bo1",
          "L0_xattn_wq2", "L0_xattn_wk2", "L0_xattn_wv2", "L0_xattn_wo2", "L0_xattn_bo2", "L0_xattn_w_geglu",
          "L0_xattn_b_geglu", "L0_xattn_w_ffout", "L0_xattn_b_ffout", "L0_xattn_ln1_g", "L0_xattn_ln1_b",
          "L0_xattn_ln2_g", "L0_xattn_ln2_b", "L0_xattn_ln3_g", "L0_xattn_ln3_b", "L1_xattn_Wq", "L1_xattn_Wk",
          "L1_xattn_Wv", "L1_xattn_Wo", "L1_xattn_gamma", "L1_xattn_beta"]


def kernel(**inputs):
    import numpy as _np
    import concourse.bacc as _bacc
    from concourse import mybir as _mybir
    from concourse.bass_utils import run_bass_kernel_spmd as _run

    nc = _bacc.Bacc("TRN2", target_bir_lowering=False, num_devices=1)
    arrays, handles = {}, {}
    for name in INPUTS:
        a = _np.ascontiguousarray(inputs[name])
        arrays[f"in_{name}"] = a
        handles[name] = nc.dram_tensor(f"in_{name}", a.shape, _mybir.dt.from_np(a.dtype), kind="ExternalInput").ap()
    out = nc.dram_tensor("out_rows", (NB, SEQ, D), F32, kind="ExternalOutput").ap()
    build(nc, handles, out)
    r = _run(nc, [arrays], core_ids=[0])
    return r.results[0]["out_rows"]
```
